# Optimizing a Trainium2 kernel written in Bass

```python
import numpy as np
import jax
import jax.numpy as jnp

def _softmax(x, axis=-1):
    return jax.nn.softmax(x, axis=axis)

def _gelu(x):
    return jax.nn.gelu(x, approximate=True)

def _silu(x):
    return jax.nn.silu(x)

def _sigmoid(x):
    return jax.nn.sigmoid(x)

def _layernorm(x, axis=-1, eps=1e-05):
    m = jnp.mean(x, axis=axis, keepdims=True)
    v = jnp.var(x, axis=axis, keepdims=True)
    return (x - m) / jnp.sqrt(v + eps)

def _scatter_add(tgt, idx, src, axis=0):
    return tgt.at[idx].add(src)

def _segment_sum(src, seg, n):
    return jax.ops.segment_sum(src, seg, n)
kernel_name = 'mk_adj_seq_d2_adj_r2_e80817'

def setup_inputs(seed: int=0):
    np.random.seed(seed)
    _w = jnp.asarray

    def _rec_inputs():
        import jax
        import jax.numpy as jnp
        _gk = jax.random.key(seed)
        x = -0.0005207 + 1.001 * jax.random.normal(jax.random.fold_in(_gk, 1), (8, 1024, 256), jnp.float32)
        _a = jax.random.bernoulli(jax.random.fold_in(_gk, 2), 0.00390625, (8, 1024, 1024))
        _a = jnp.logical_or(_a, jnp.eye(1024, dtype=bool))
        adj = _a.astype(jnp.int32)
        return (x, adj)
    x, adj = _rec_inputs()

    def _L0_gnn_setup():
        import jax, jax.numpy as jnp
        import numpy as np
        B, S, D, H = (2, 1024, 256, 8)
        HD = D // H
        EPS = 1e-05

        def _ln(x, g, b):
            mu = jnp.mean(x, axis=-1, keepdims=True)
            var = jnp.mean((x - mu) ** 2, axis=-1, keepdims=True)
            return (x - mu) * jax.lax.rsqrt(var + EPS) * g + b
        key = jax.random.key(seed)
        ks = jax.random.split(key, 16)
        x = jax.random.normal(ks[0], (B, S, D), dtype=jnp.float32)
        adj = jax.random.randint(ks[1], (B, S, S), 0, 2, dtype=jnp.int32)
        adj = adj.at[:, jnp.arange(S), jnp.arange(S)].set(1)
        edge_attr = jax.random.normal(ks[2], (B, S, S), dtype=jnp.float32)
        sc = 1.0 / np.sqrt(D)
        p = lambda k, shp: jax.random.normal(k, shp, dtype=jnp.float32) * sc
        return {'x': x, 'adj_matrix': adj, 'edge_attr_matrix': edge_attr, 'ln1_g': jnp.ones((D,)), 'ln1_b': jnp.zeros((D,)), 'ln2_g': jnp.ones((D,)), 'ln2_b': jnp.zeros((D,)), 'wq': p(ks[3], (D, D)), 'bq': jnp.zeros((D,)), 'wk': p(ks[4], (D, D)), 'bk': jnp.zeros((D,)), 'wv': p(ks[5], (D, D)), 'bv': jnp.zeros((D,)), 'wo': p(ks[6], (D, D)), 'bo': jnp.zeros((D,)), 'w1': p(ks[7], (D, 4 * D)), 'b1': jnp.zeros((4 * D,)), 'w2': p(ks[8], (4 * D, D)), 'b2': jnp.zeros((D,))}
    _L0_gnn_all = _L0_gnn_setup()
    _L0_gnn_in = {k: v for k, v in _L0_gnn_all.items() if k in ('ln1_g', 'ln1_b', 'ln2_g', 'ln2_b', 'wq', 'bq', 'wk', 'bk', 'wv', 'bv', 'wo', 'bo', 'w1', 'b1', 'w2', 'b2')}
    del _L0_gnn_all

    def _L1_gnn_setup():
        import jax, jax.numpy as jnp
        import numpy as np
        B, N, H, D = (8, 512, 256, 4)
        EPS = 1e-08
        LN_EPS = 1e-05

        def _linear(x, W, b):
            return x @ W.T + b
        key = jax.random.key(seed)
        ks = jax.random.split(key, 20)
        inp = {'adj': jax.random.randint(ks[0], (B, N, N), 0, D + 1, dtype=jnp.int32), 'relative_pos': jax.random.randint(ks[1], (B, N, N), 0, 16, dtype=jnp.int32), 'hid': jax.random.normal(ks[2], (B, N, H), dtype=jnp.float32), 'Wd': jax.random.normal(ks[3], (H, D * H), dtype=jnp.float32) * (1.0 / np.sqrt(D * H)), 'bd': jnp.zeros((H,), jnp.float32)}
        s = 1.0 / np.sqrt(H)
        for i, nm in enumerate(['ri', 'rh', 'zi', 'zh', 'ni', 'nh']):
            inp['W' + nm] = jax.random.normal(ks[4 + i], (H, H), dtype=jnp.float32) * s
            inp['b' + nm] = jnp.zeros((H,), jnp.float32)
        inp['gamma'] = jnp.ones((H,), jnp.float32)
        inp['beta'] = jnp.zeros((H,), jnp.float32)
        return inp
    _L1_gnn_all = _L1_gnn_setup()
    _L1_gnn_in = {k: v for k, v in _L1_gnn_all.items() if k in ('Wd', 'bd', 'Wri', 'bri', 'Wrh', 'brh', 'Wzi', 'bzi', 'Wzh', 'bzh', 'Wni', 'bni', 'Wnh', 'bnh', 'gamma', 'beta')}
    del _L1_gnn_all
    return {'x': x, 'adj': adj, 'L0_gnn_ln1_g': _L0_gnn_in['ln1_g'], 'L0_gnn_ln1_b': _L0_gnn_in['ln1_b'], 'L0_gnn_ln2_g': _L0_gnn_in['ln2_g'], 'L0_gnn_ln2_b': _L0_gnn_in['ln2_b'], 'L0_gnn_wq': _L0_gnn_in['wq'], 'L0_gnn_bq': _L0_gnn_in['bq'], 'L0_gnn_wk': _L0_gnn_in['wk'], 'L0_gnn_bk': _L0_gnn_in['bk'], 'L0_gnn_wv': _L0_gnn_in['wv'], 'L0_gnn_bv': _L0_gnn_in['bv'], 'L0_gnn_wo': _L0_gnn_in['wo'], 'L0_gnn_bo': _L0_gnn_in['bo'], 'L0_gnn_w1': _L0_gnn_in['w1'], 'L0_gnn_b1': _L0_gnn_in['b1'], 'L0_gnn_w2': _L0_gnn_in['w2'], 'L0_gnn_b2': _L0_gnn_in['b2'], 'L1_gnn_Wd': _L1_gnn_in['Wd'], 'L1_gnn_bd': _L1_gnn_in['bd'], 'L1_gnn_Wri': _L1_gnn_in['Wri'], 'L1_gnn_bri': _L1_gnn_in['bri'], 'L1_gnn_Wrh': _L1_gnn_in['Wrh'], 'L1_gnn_brh': _L1_gnn_in['brh'], 'L1_gnn_Wzi': _L1_gnn_in['Wzi'], 'L1_gnn_bzi': _L1_gnn_in['bzi'], 'L1_gnn_Wzh': _L1_gnn_in['Wzh'], 'L1_gnn_bzh': _L1_gnn_in['bzh'], 'L1_gnn_Wni': _L1_gnn_in['Wni'], 'L1_gnn_bni': _L1_gnn_in['bni'], 'L1_gnn_Wnh': _L1_gnn_in['Wnh'], 'L1_gnn_bnh': _L1_gnn_in['bnh'], 'L1_gnn_gamma': _L1_gnn_in['gamma'], 'L1_gnn_beta': _L1_gnn_in['beta']}

def reference(x, adj, L0_gnn_ln1_g, L0_gnn_ln1_b, L0_gnn_ln2_g, L0_gnn_ln2_b, L0_gnn_wq, L0_gnn_bq, L0_gnn_wk, L0_gnn_bk, L0_gnn_wv, L0_gnn_bv, L0_gnn_wo, L0_gnn_bo, L0_gnn_w1, L0_gnn_b1, L0_gnn_w2, L0_gnn_b2, L1_gnn_Wd, L1_gnn_bd, L1_gnn_Wri, L1_gnn_bri, L1_gnn_Wrh, L1_gnn_brh, L1_gnn_Wzi, L1_gnn_bzi, L1_gnn_Wzh, L1_gnn_bzh, L1_gnn_Wni, L1_gnn_bni, L1_gnn_Wnh, L1_gnn_bnh, L1_gnn_gamma, L1_gnn_beta):
    import jax
    import jax.numpy as jnp

    def _L0_gnn_ref(x, adj_matrix, edge_attr_matrix, ln1_g, ln1_b, ln2_g, ln2_b, wq, bq, wk, bk, wv, bv, wo, bo, w1, b1, w2, b2):
        import jax, jax.numpy as jnp
        import numpy as np
        B, S, D, H = (2, 1024, 256, 8)
        HD = D // H
        EPS = 1e-05

        def _ln(x, g, b):
            mu = jnp.mean(x, axis=-1, keepdims=True)
            var = jnp.mean((x - mu) ** 2, axis=-1, keepdims=True)
            return (x - mu) * jax.lax.rsqrt(var + EPS) * g + b
        b, s, d = x.shape
        residual = x
        nx = _ln(x, ln1_g, ln1_b)
        q = (nx @ wq + bq).reshape(b, s, H, HD).transpose(0, 2, 1, 3)
        k = (nx @ wk + bk).reshape(b, s, H, HD).transpose(0, 2, 1, 3)
        v = (nx @ wv + bv).reshape(b, s, H, HD).transpose(0, 2, 1, 3)
        adjf = adj_matrix.astype(jnp.float32)
        bias = jnp.where(adj_matrix > 0, 0.1 * edge_attr_matrix * adjf, -jnp.inf)[:, None]
        scores = jnp.einsum('bhqd,bhkd->bhqk', q, k) / np.sqrt(HD) + bias
        attn = jax.nn.softmax(scores, axis=-1)
        out = jnp.einsum('bhqk,bhkd->bhqd', attn, v)
        out = out.transpose(0, 2, 1, 3).reshape(b, s, d)
        x1 = residual + (out @ wo + bo)
        n2 = _ln(x1, ln2_g, ln2_b)
        mlp = jax.nn.gelu(n2 @ w1 + b1, approximate=False) @ w2 + b2
        return x1 + mlp

    def _L1_gnn_ref(adj, relative_pos, hid, Wd, bd, Wri, bri, Wrh, brh, Wzi, bzi, Wzh, bzh, Wni, bni, Wnh, bnh, gamma, beta):
        import jax, jax.numpy as jnp
        import numpy as np
        B, N, H, D = (8, 512, 256, 4)
        EPS = 1e-08
        LN_EPS = 1e-05

        def _linear(x, W, b):
            return x @ W.T + b
        dt = hid.dtype
        labels = jnp.arange(1, D + 1, dtype=adj.dtype)
        mask = (adj[None] == labels[:, None, None, None]).astype(dt)
        weight = mask / (jnp.sum(mask, axis=-1, keepdims=True) + EPS)
        agg = jnp.einsum('dbmn,bnh->bmdh', weight, hid).reshape(hid.shape[0], hid.shape[1], D * H)
        out = jax.nn.relu(_linear(agg, Wd, bd))
        r = jax.nn.sigmoid(_linear(out, Wri, bri) + _linear(hid, Wrh, brh))
        z = jax.nn.sigmoid(_linear(out, Wzi, bzi) + _linear(hid, Wzh, bzh))
        n = jnp.tanh(_linear(out, Wni, bni) + r * _linear(hid, Wnh, bnh))
        out = (1.0 - z) * n + z * hid
        mu = jnp.mean(out, axis=-1, keepdims=True)
        var = jnp.var(out, axis=-1, keepdims=True)
        return (out - mu) / jnp.sqrt(var + LN_EPS) * gamma + beta
    x = _L0_gnn_ref(x, adj, adj, L0_gnn_ln1_g, L0_gnn_ln1_b, L0_gnn_ln2_g, L0_gnn_ln2_b, L0_gnn_wq, L0_gnn_bq, L0_gnn_wk, L0_gnn_bk, L0_gnn_wv, L0_gnn_bv, L0_gnn_wo, L0_gnn_bo, L0_gnn_w1, L0_gnn_b1, L0_gnn_w2, L0_gnn_b2)
    x = _L1_gnn_ref(adj, adj, x, L1_gnn_Wd, L1_gnn_bd, L1_gnn_Wri, L1_gnn_bri, L1_gnn_Wrh, L1_gnn_brh, L1_gnn_Wzi, L1_gnn_bzi, L1_gnn_Wzh, L1_gnn_bzh, L1_gnn_Wni, L1_gnn_bni, L1_gnn_Wnh, L1_gnn_bnh, L1_gnn_gamma, L1_gnn_beta)
    return x

_drawn_inputs = setup_inputs


def setup_inputs(seed=0):
    import zlib

    import numpy as np

    out = dict(_drawn_inputs(seed))
    spreads = {'L0_gnn_ln1_g': (1.0, 0.2),
     'L0_gnn_ln1_b': (0.0, 0.1),
     'L0_gnn_ln2_g': (1.0, 0.2),
     'L0_gnn_ln2_b': (0.0, 0.1),
     'L0_gnn_bq': (0.0, 0.1),
     'L0_gnn_bk': (0.0, 0.8),
     'L0_gnn_bv': (0.0, 0.1),
     'L0_gnn_bo': (0.0, 0.1),
     'L0_gnn_b1': (0.0, 0.1),
     'L0_gnn_b2': (0.0, 0.1),
     'L1_gnn_bd': (0.0, 0.1),
     'L1_gnn_bri': (0.0, 0.8),
     'L1_gnn_brh': (0.0, 0.8),
     'L1_gnn_bzi': (0.0, 0.1),
     'L1_gnn_bzh': (0.0, 0.1),
     'L1_gnn_bni': (0.0, 0.1),
     'L1_gnn_bnh': (0.0, 0.443),
     'L1_gnn_gamma': (1.0, 0.2),
     'L1_gnn_beta': (0.0, 0.1)}
    factors = {}
    for name, (base, spread) in spreads.items():
        noise = np.random.default_rng([zlib.crc32(name.encode()), seed]).standard_normal(out[name].shape)
        drawn = base * np.exp(spread * noise) if base else spread * noise
        out[name] = jnp.asarray(drawn.astype(out[name].dtype))
    for name, factor in factors.items():
        out[name] = (out[name] * factor).astype(out[name].dtype)
    return out
```

```python
from contextlib import ExitStack

import numpy as np

import concourse.bass as bass
from concourse import mybir

ALU = mybir.AluOpType
ACT = mybir.ActivationFunctionType
F32 = mybir.dt.float32
F32R = mybir.dt.float32r
I32 = mybir.dt.int32

P = 128
NEG = -1.0e30
BIG = 3.0e38
LN_EPS = 1e-5
AGG_EPS = 1e-8
HI, LO = 0, 1


class PsumPlan:

    def __init__(self):
        self.place, self.uses = {}, {}

    def add(self, key, unit):
        self.uses[unit] = self.uses.get(unit, 0) + 1
        self.place[key] = (unit, self.uses[unit])


def gated_graph_layers(nc, x, adj, adj_t, ln1_g, ln1_b, ln2_g, ln2_b, wq, bq, wk, bk, wv, bv, wo, bo, w1, b1,
                       w2, b2, wd_t, bd, wri_t, bri, wrh_t, brh, wzi_t, bzi, wzh_t, bzh, wni_t, bni, wnh_t, bnh,
                       gamma, beta, out):
    NBATCH, S, D = x.shape
    HEADS = 8
    HD = D // HEADS
    TT = S // P
    KD = D // P
    NBLK = S // 512
    FF = w1.shape[1]
    FM = FF // P
    LABELS = wd_t.shape[0] // D
    KA = LABELS * KD
    SLOTS = TT * HEADS
    UNITS = SLOTS // 4
    QSCALE = float(1.0 / np.sqrt(HD))

    plan = PsumPlan()
    for blk in range(NBLK):
        for k in range(KD):
            plan.add(("z1", blk, k), f"T{k}")
    for blk in range(NBLK):
        for m in range(2 * KD):
            plan.add(("qk", blk, m), f"R{m % 2}")
    for t in range(TT):
        plan.add(("v", t), "VM"[t % 2])
    for s in range(SLOTS):
        plan.add(("s", s), f"R{s % 2}")
        for i in range(2):
            plan.add(("t", s, i), f"T{i}")
    for u in range(UNITS):
        plan.add(("pv", u), "V")
        plan.add(("otok", u), "M")
        plan.add(("ot", u), "M")
    for t in range(TT):
        plan.add(("wo", t), f"R{t % 2}")
    for blk in range(NBLK):
        for k in range(KD):
            plan.add(("z2", blk, k), f"T{k}")
    for c in range(TT // 2):
        for m in range(FM):
            plan.add(("w1", c, m), f"R{m % 2}")
        for t in (2 * c, 2 * c + 1):
            plan.add(("w2", t), "VM"[t % 2])
    for blk in range(NBLK):
        for k in range(KD):
            plan.add(("ht", blk, k), f"T{k}")
    for t in range(TT):
        for i in range(2):
            plan.add(("agg", t, i), f"R{i}")
            plan.add(("at", t, i), f"T{i}")
    for c in range(TT // 2):
        for m in range(KD):
            plan.add(("wd", c, m), "VM"[m])
        for t in (2 * c, 2 * c + 1):
            plan.add(("rz", t), "V")
            plan.add(("n", t), "M")

    splits = {}
    for key in ([("z1", b_, k) for b_ in range(NBLK) for k in range(KD)]
                + [("qk", b_, m) for b_ in range(NBLK) for m in range(2 * KD)]
                + [("z2", b_, k) for b_ in range(NBLK) for k in range(KD)]
                + [("w1", c, m) for c in range(TT // 2) for m in range(FM)]
                + [("wd", c, m) for c in range(TT // 2) for m in range(KD)]):
        splits[key] = len(splits)

    ctx = ExitStack()
    with ctx:
        def sb(name, shape, dt):
            return ctx.enter_context(nc.sbuf_tensor(name, shape, dt))

        def sem(name):
            return ctx.enter_context(nc.semaphore(name))

        WP = 3 * KD * D + KD * D + KD * FF + FM * D
        weights = sb("weights", [P, 2, WP], F32R)
        LATE = KA * D + 2 * KD * 2 * D + 2 * KD * D
        shared_late = sb("late_or_stacks", [P, 2 * LATE], F32R)
        act_t = sb("act_t", [P, 2, KD, S], F32R)
        xin = sb("xin", [P, TT, D], F32)
        x1 = sb("x1", [P, TT, D], F32)
        z = sb("z", [P, 4, D], F32)
        tmp = sb("tmp", [P, 2, 512], F32)
        cols = sb("cols", [P, 24], F32)
        ident = sb("ident", [P, P], F32)
        ones = sb("ones", [P, P], F32R)
        rows = sb("rows", [P, 3 * D], F32R)
        gamma_b = sb("gamma_b", [P, D], F32)
        beta_b = sb("beta_b", [P, D], F32)
        stats = sb("stats", [P, TT, 6], F32)
        mv = sb("mv", [P, TT, 2], F32)
        sd = sb("sd", [P, TT], F32)
        rstd = sb("rstd", [P, TT], F32)
        epsc = sb("epsc", [P, 1], F32)
        negmax = sb("negmax", [P, SLOTS], F32)
        rowsum = sb("rowsum", [P, SLOTS], F32)
        rinv = sb("rinv", [P, SLOTS], F32)
        winv = sb("winv", [P, TT, LABELS], F32)
        adj_i = sb("adj_i", [P, 2, S], I32)
        edge = sb("edge", [P, LABELS * D], F32)
        with ExitStack() as a:
            pt = a.enter_context(nc.sbuf_tensor("pt", [P, 2, 4, TT, P], F32))
            vtok = a.enter_context(nc.sbuf_tensor("vtok", [P, TT, D], F32))
            prob = a.enter_context(nc.sbuf_tensor("prob", [P, 2, S], F32))
            bias = a.enter_context(nc.sbuf_tensor("bias", [P, 2, S], F32))
            ots = a.enter_context(nc.sbuf_tensor("ots", [P, 2, P], F32))
            otok = a.enter_context(nc.sbuf_tensor("otok", [P, 2, 4, HD], F32))
        with ExitStack() as a:
            qk_parts = a.enter_context(nc.sbuf_tensor("qk_parts", [P, NBLK, 2 * KD, 2, 512], F32R))
        with ExitStack() as a:
            n2_mask = a.enter_context(nc.sbuf_tensor("n2_mask", [P, 4 * S], F32R))
            wide = a.enter_context(nc.sbuf_tensor("wide", [P, 2, 8, 256], F32R))
            hid_r = a.enter_context(nc.sbuf_tensor("hid_r", [P, TT, 2, D + 2], F32R))
            out_t = a.enter_context(nc.sbuf_tensor("out_t", [P, 2, KD, 256], F32R))
            tn = a.enter_context(nc.sbuf_tensor("tn", [P, 2, D], F32))
            cand = a.enter_context(nc.sbuf_tensor("cand", [P, 2, D], F32))
        attn_end = ctx.enter_context(nc.sbuf_tensor("phase_area", [P, 2 * 4 * TT * P + 3 * 2048 + 512], F32))

        psum = ctx.enter_context(nc.psum_tensor("psum", [P, 8 * 512], F32))
        unit_at = {"R0": psum[:, 0:1024], "R1": psum[:, 1024:2048], "T0": psum[:, 2048:2560],
                   "T1": psum[:, 2560:3072], "V": psum[:, 3072:3584], "M": psum[:, 3584:4096]}

        def room(key):
            return unit_at[plan.place[key][0]]

        o = 0
        w_at = {}
        for name, k, n in (("q", KD, D), ("k", KD, D), ("v", KD, D), ("o", KD, D), ("1", KD, FF), ("2", FM, D)):
            w_at[name] = weights[:, :, o:o + k * n].rearrange("p h (k n) -> p h k n", k=k)
            o += k * n
        late = shared_late[:, :].rearrange("p (h n) -> p h n", h=2)
        o = 0
        for name, k, n in (("d", KA, D), ("rzi", KD, 2 * D), ("rzh", KD, 2 * D), ("ni", KD, D), ("nh", KD, D)):
            w_at[name] = late[:, :, o:o + k * n].rearrange("p h (k n) -> p h k n", k=k)
            o += k * n
        kstack = shared_late[0:3 * HD, 0:HEADS * S].rearrange("p (h s) -> p h s", h=HEADS)
        qstack = shared_late[0:3 * HD, HEADS * S:HEADS * S + 2 * HEADS * P].rearrange("p (r h q) -> p r h q", r=2, h=HEADS)
        n2_t = n2_mask[:, :].rearrange("p (h k s) -> p h k s", h=2, k=KD)
        mask = n2_mask[:, :].rearrange("p (r t m) -> p r t m", r=4, t=TT)
        gates = z[:, :, :].rearrange("p (r a) d -> p r (a d)", r=2)
        agg_s = edge[:, :]
        col = {}
        for i, (name, k) in enumerate((("bq", KD), ("bk", KD), ("g1", KD), ("b1n", KD), ("g2", KD), ("b2n", KD),
                                       ("b1", FM), ("bd", KD))):
            at = sum(k_ for _, k_ in (("bq", KD), ("bk", KD), ("g1", KD), ("b1n", KD), ("g2", KD), ("b2n", KD),
                                      ("b1", FM), ("bd", KD))[:i])
            col[name] = cols[:, at:at + k]
        row_rz, row_v = rows[0:2, 0:2 * D], rows[0:2, 2 * D:3 * D]
        row_o, row_2 = rows[32:34, 0:D], rows[32:34, D:2 * D]
        row_ni, row_nh = rows[64:66, 0:D], rows[64:66, D:2 * D]

        late_d = nc.dram_tensor("late_weights", [P, 2, LATE], F32).ap()
        qk_d = nc.dram_tensor("qk_parts_d", [2, 2, D, S], F32).ap()

        full = {u: sem(f"full_{u}") for u in unit_at}
        free = {u: sem(f"free_{u}") for u in unit_at}
        x_in = sem("x_in")
        adj_in = [sem(f"adj_in{i}") for i in range(2)]
        qk_stored = sem("qk_stored")
        ks_in = sem("ks_in")
        qs_in = [sem(f"qs_in{i}") for i in range(2)]
        late_in = sem("late_in")
        y_out = sem("y_out")
        ln_mv = sem("ln_mv")
        ln_sd = sem("ln_sd")
        z_ready = sem("z_ready")
        split_done = sem("split_done")
        dve_step = sem("dve_step")
        pool_step = sem("pool_step")
        bias_ready = sem("bias_ready")
        scored = sem("scored")
        ot_hi = sem("ot_hi")
        hid_parts = sem("hid_parts")
        ht_hi = sem("ht_hi")
        mask_ready = sem("mask_ready")
        w_ready = sem("w_ready")
        agg_hi = sem("agg_hi")
        tanh_done = sem("tanh_done")
        gru_out = sem("gru_out")
        z3_ready = sem("z3_ready")
        y_ready = sem("y_ready")
        batch_sems = [*full.values(), *free.values(), x_in, *adj_in, qk_stored, ks_in, *qs_in, late_in, y_out,
                      ln_mv, ln_sd, z_ready, split_done, dve_step, pool_step, bias_ready, scored, ot_hi, hid_parts,
                      ht_hi, mask_ready, w_ready, agg_hi, tanh_done, gru_out, z3_ready, y_ready]
        w_in = sem("w_in")
        w_in2 = sem("w_in2")
        w_split = sem("w_split")
        w_aux = sem("w_aux")
        rows_in = sem("rows_in")
        late_out = sem("late_out")
        w_ident = sem("w_ident")

        def full_of(eng, key):
            unit, n = plan.place[key]
            eng.wait_ge(full[unit], n)

        def free_of(eng, key):
            unit, n = plan.place[key]
            eng.wait_ge(free[unit], n)

        def unit_clear(eng, key):
            unit, n = plan.place[key]
            if n > 1:
                eng.wait_ge(free[unit], n - 1)

        def full_sem(key):
            return full[plan.place[key][0]]

        def free_sem(key):
            return free[plan.place[key][0]]

        raw = pt[:, :, :, :, :].rearrange("p a b c d -> p (a b c d)")

        with nc.Block() as block:
            @block.sync
            def _(sp):
                o = 0
                for w, k, n in ((wq, KD, D), (wk, KD, D), (wv, KD, D), (wo, KD, D), (w1, KD, FF), (w2, FM, D)):
                    sp.dma_start(raw[:, o:o + k * n].rearrange("p (k n) -> p k n", k=k),
                                 w.rearrange("(k p) n -> p k n", p=P)).then_inc(w_in, 16)
                    o += k * n
                with nc.allow_non_contiguous_dma(reason="biases"):
                    for name, v in (("bq", bq), ("bk", bk), ("g1", ln1_g), ("b1n", ln1_b), ("g2", ln2_g),
                                    ("b2n", ln2_b), ("b1", b1), ("bd", bd)):
                        sp.dma_start(col[name], v.rearrange("(k p) -> p k", p=P)).then_inc(w_aux, 16)
                xrow = xin[0:1, :, :].rearrange("p t d -> p (t d)")
                x1row = x1[0:1, :, :].rearrange("p t d -> p (t d)")
                for i, v in enumerate((bri, bzi, bv, bo, b2, bni, bnh)):
                    sp.dma_start(x1row[:, i * D:(i + 1) * D], v.rearrange("(a n) -> a n", a=1)).then_inc(w_aux, 16)
                for i, v in enumerate((brh, bzh)):
                    sp.dma_start(xrow[:, i * D:(i + 1) * D], v.rearrange("(a n) -> a n", a=1)).then_inc(w_aux, 16)
                sp.dma_start(gamma_b[:, :], gamma.rearrange("(a n) -> a n", a=1).broadcast_to([P, D])).then_inc(w_aux, 16)
                sp.dma_start(beta_b[:, :], beta.rearrange("(a n) -> a n", a=1).broadcast_to([P, D])).then_inc(w_aux, 16)
                sp.wait_ge(w_split, 2)
                o = 0
                sp.dma_start(raw[:, 0:KA * D].rearrange("p (k n) -> p k n", k=KA),
                             wd_t.rearrange("(k p) n -> p k n", p=P)).then_inc(w_in2, 16)
                o = KA * D
                for pair in ((wri_t, wzi_t), (wrh_t, wzh_t), (wni_t,), (wnh_t,)):
                    n = len(pair) * D
                    dst = raw[:, o:o + KD * n].rearrange("p (k n) -> p k n", k=KD)
                    for i, w in enumerate(pair):
                        sp.dma_start(dst[:, :, i * D:(i + 1) * D], w.rearrange("(k p) n -> p k n", p=P)).then_inc(w_in2, 16)
                    o += KD * n
                sp.wait_ge(w_aux, 16 * 19 + 3)
                parts = act_t[0:1, :, :, :].rearrange("p h k s -> p h (k s)").bitcast(F32)
                for part in (HI, LO):
                    for base, at, a_, n in ((0, 0, 0, 3 * D), (32, 0, 3 * D, 2 * D), (64, 0, 5 * D, 2 * D)):
                        sp.dma_start(rows[base + part:base + part + 1, at:at + n].bitcast(F32),
                                     parts[:, part, a_:a_ + n]).then_inc(rows_in, 16)
                sp.wait_ge(w_split, 4)
                sp.dma_start(late_d, late.bitcast(F32)).then_inc(late_out, 16)
                sp.wait_ge(rows_in, 16 * 6)
                sp.wait_ge(late_out, 16)

            @block.vector
            def _(dve):
                dve.wait_ge(w_in, 16 * 6)
                dve.tensor_copy(weights[:, HI, :], raw[:, 0:WP]).then_inc(w_split, 1)
                dve.wait_ge(w_split, 1)
                dve.tensor_tensor(weights[:, LO, :], raw[:, 0:WP], weights[:, HI, :].bitcast(F32), ALU.subtract).then_inc(w_split, 1)
                dve.wait_ge(w_aux, 16 * 19)
                x1row = x1[0:1, :, :].rearrange("p t d -> p (t d)")
                xrow = xin[0:1, :, :].rearrange("p t d -> p (t d)")
                parts = act_t[0:1, :, :, :].rearrange("p h k s -> p h (k s)")
                dve.tensor_scalar(col["bq"], col["bq"], QSCALE, None, ALU.mult).then_inc(w_aux, 1)
                dve.wait_ge(w_aux, 16 * 19 + 1)
                dve.tensor_tensor(x1row[:, 0:2 * D], x1row[:, 0:2 * D], xrow[:, 0:2 * D], ALU.add).then_inc(w_aux, 1)
                dve.wait_ge(w_aux, 16 * 19 + 2)
                dve.tensor_copy(parts[:, HI, 0:7 * D], x1row[:, 0:7 * D]).then_inc(dve_step, 1)
                dve.wait_ge(dve_step, 1)
                dve.tensor_tensor(parts[:, LO, 0:7 * D], x1row[:, 0:7 * D], parts[:, HI, 0:7 * D].bitcast(F32),
                                  ALU.subtract).then_inc(w_aux, 1)
                dve.wait_ge(w_in2, 16 * 7)
                dve.tensor_copy(late[:, HI, :], raw[:, 0:LATE]).then_inc(w_split, 1)
                dve.wait_ge(w_split, 3)
                dve.tensor_tensor(late[:, LO, :], raw[:, 0:LATE], late[:, HI, :].bitcast(F32), ALU.subtract).then_inc(w_split, 1)

            @block.gpsimd
            def _(pool):
                pool.memset(ones[:, :].bitcast(F32), 1.0)
                pool.memset(epsc[:, :], LN_EPS)
                pool.memset(ident[:, :], 0.0).then_inc(w_ident, 1)
                pool.wait_ge(w_ident, 1)
                pool.affine_select(out=ident[:, :], in_=ident[:, :], compare_op=ALU.not_equal, fill=1.0, base=0,
                                   pattern=[[-1, P]], channel_multiplier=1).then_inc(w_ident, 1)

        with nc.Fori(0, NBATCH) as b:
            nc.all_engine_barrier()
            for s_ in batch_sems:
                nc.sync.sem_clear(s_)
            nc.all_engine_barrier()
            with nc.Block() as block:
                x_b = x[b].rearrange("(t p) d -> p t d", p=P)
                adj_b = adj[b].rearrange("(t p) k -> t p k", p=P)
                adjt_b = adj_t[b].rearrange("(n p) (t m) -> t p n m", p=P, m=P)
                out_b = out[b].rearrange("(t p) d -> t p d", p=P)

                @block.sync
                def _(sp):
                    sp.dma_start(xin[:, :, :], x_b).then_inc(x_in, 16)
                    for i in range(2):
                        sp.dma_start(adj_i[:, i, :], adj_b[i]).then_inc(adj_in[i], 16)
                    for blk in range(NBLK):
                        for m in range(2 * KD):
                            sp.wait_ge(split_done, splits["qk", blk, m] + 1)
                            dst = qk_d[m // KD, :, (m % KD) * P:(m % KD + 1) * P, blk * 512:(blk + 1) * 512]
                            sp.dma_start(dst.rearrange("h p s -> p h s"),
                                         qk_parts[:, blk, m, :, :].bitcast(F32)).then_inc(qk_stored, 16)
                    sp.wait_ge(qk_stored, 16 * NBLK * 2 * KD)
                    for r, part in enumerate((HI, LO, HI)):
                        sp.dma_start(kstack[r * HD:(r + 1) * HD, :, :].bitcast(F32),
                                     qk_d[1, part].rearrange("(h d) s -> d h s", d=HD)).then_inc(ks_in, 16)

                    def load_queries(t):
                        for r, part in enumerate((HI, HI, LO)):
                            sp.dma_start(qstack[r * HD:(r + 1) * HD, t % 2, :, :].bitcast(F32),
                                         qk_d[0, part, :, t * P:(t + 1) * P].rearrange("(h d) s -> d h s", d=HD)
                                         ).then_inc(qs_in[t % 2], 16)

                    load_queries(0)
                    load_queries(1)
                    for t in range(2, TT):
                        sp.wait_ge(bias_ready, t - 1)
                        sp.dma_start(adj_i[:, t % 2, :], adj_b[t]).then_inc(adj_in[t % 2], 16)
                        full_of(sp, ("s", HEADS * (t - 1) - 1))
                        load_queries(t)
                    for t in range(2):
                        sp.wait_ge(bias_ready, TT - 1 + t)
                        sp.dma_start(adj_i[:, t, :].rearrange("p (n m) -> p n m", m=P), adjt_b[t]).then_inc(adj_in[t], 16)
                    full_of(sp, ("s", SLOTS - 1))
                    for part in (HI, LO):
                        sp.dma_start(late[:, part, :].bitcast(F32), late_d[:, part, :]).then_inc(late_in, 16)
                    for t in range(2, TT):
                        sp.wait_ge(mask_ready, LABELS * (t - 1))
                        sp.dma_start(adj_i[:, t % 2, :].rearrange("p (n m) -> p n m", m=P), adjt_b[t]).then_inc(adj_in[t % 2], 16)
                    for t in range(TT):
                        sp.wait_ge(y_ready, t + 1)
                        sp.dma_start(out_b[t], x1[:, t, :]).then_inc(y_out, 16)
                    sp.wait_ge(y_out, 16 * TT)

                @block.gpsimd
                def _(pool):
                    steps = [0]

                    def link(ins):
                        steps[0] += 1
                        ins.then_inc(pool_step, 1)
                        pool.wait_ge(pool_step, steps[0])

                    def edge_bias(t):
                        pool.wait_ge(adj_in[t % 2], 16 * (t // 2 + 1))
                        if t >= 2:
                            pool.wait_ge(scored, HEADS * (t - 1))
                        if t >= 1:
                            pool.wait_ge(bias_ready, t)
                        pool.tensor_scalar(bias[:, t % 2, :], adj_i[:, t % 2, :], 0.0, NEG, ALU.is_le, ALU.mult)
                        link(pool.tensor_scalar(edge[:, :], adj_i[:, t % 2, :], 1.0, None, ALU.mult))
                        link(pool.tensor_tensor(edge[:, :], edge[:, :], edge[:, :], ALU.mult))
                        link(pool.tensor_scalar(edge[:, :], edge[:, :], 0.1, None, ALU.mult))
                        pool.tensor_tensor(bias[:, t % 2, :], bias[:, t % 2, :], edge[:, :], ALU.add).then_inc(bias_ready, 1)

                    for t in range(TT):
                        edge_bias(t)

                    def hid_rows(t):
                        free_of(pool, ("w2", t))
                        link(pool.tensor_copy(hid_r[:, t, HI, 0:D], x1[:, t, :]))
                        pool.tensor_tensor(hid_r[:, t, LO, 0:D], x1[:, t, :], hid_r[:, t, HI, 0:D].bitcast(F32),
                                           ALU.subtract).then_inc(hid_parts, 1)

                    def masks(t):
                        pool.wait_ge(adj_in[t % 2], 16 * (TT // 2 + t // 2 + 1))
                        for d in range(LABELS):
                            if t == 0:
                                full_of(pool, ("w1", TT // 2 - 1, FM - 1))
                            else:
                                full_of(pool, ("agg", t - 1, d // 2))
                            pool.tensor_scalar(mask[:, d, :, :], adj_i[:, t % 2, :].rearrange("p (n m) -> p n m", m=P),
                                               float(d + 1), None, ALU.is_equal).then_inc(mask_ready, 1)

                    def blend(t):
                        pool.wait_ge(tanh_done, t + 1)
                        link(pool.tensor_tensor(tn[:, t % 2, :], x1[:, t, :], cand[:, t % 2, :], ALU.subtract))
                        link(pool.tensor_tensor(tn[:, t % 2, :], tn[:, t % 2, :], gates[:, t % 2, D:2 * D], ALU.mult))
                        pool.tensor_tensor(x1[:, t, :], cand[:, t % 2, :], tn[:, t % 2, :], ALU.add).then_inc(gru_out, 1)

                    full_of(pool, ("w1", 0, FM - 1))
                    pool.memset(hid_r[:, :, :, D:D + 2].bitcast(F32), 0.0).then_inc(pool_step, 1)
                    steps[0] += 1
                    pool.wait_ge(pool_step, steps[0])
                    link(pool.memset(hid_r[:, :, HI, D:D + 1].bitcast(F32), 1.0))
                    for t in range(TT - 2):
                        hid_rows(t)
                    masks(0)
                    hid_rows(TT - 2)
                    hid_rows(TT - 1)
                    for t in range(1, TT):
                        masks(t)
                        if t >= 4 and t % 2 == 0:
                            blend(t - 4)
                            blend(t - 3)
                    for t in range(TT - 4, TT):
                        blend(t)
                    for t in range(TT):
                        pool.wait_ge(z3_ready, t + 1)
                        link(pool.tensor_tensor(x1[:, t, :], x1[:, t, :], gamma_b[:, :], ALU.mult))
                        pool.tensor_tensor(x1[:, t, :], x1[:, t, :], beta_b[:, :], ALU.add).then_inc(y_ready, 1)

                @block.scalar
                def _(act):
                    def deviation(n):
                        act.wait_ge(ln_mv, n)
                        act.activation(sd[:, :], mv[:, :, 1], ACT.Sqrt, bias=epsc[:, 0:1]).then_inc(ln_sd, 1)

                    def to_tmp(key, func, n, **how):
                        j = splits[key]
                        if j >= 2:
                            act.wait_ge(split_done, j - 1)
                        full_of(act, key)
                        act.activation(tmp[:, j % 2, 0:n], room(key)[:, 0:n], func, **how).then_inc(free_sem(key), 1)

                    deviation(1)
                    for blk in range(NBLK):
                        for k in range(KD):
                            to_tmp(("z1", blk, k), ACT.Identity, 512, scale=col["g1"][:, k:k + 1], bias=col["b1n"][:, k:k + 1])
                    for blk in range(NBLK):
                        for m in range(2 * KD):
                            name, scale = (("bq", QSCALE), ("bk", 1.0))[m // KD]
                            to_tmp(("qk", blk, m), ACT.Identity, 512, scale=scale, bias=col[name][:, m % KD:m % KD + 1])
                    for t in range(TT):
                        full_of(act, ("v", t))
                        act.activation(vtok[:, t, :], room(("v", t))[:, 0:D], ACT.Copy).then_inc(free_sem(("v", t)), 1)

                    for s in range(SLOTS + 8):
                        if s < SLOTS:
                            act.wait_ge(scored, s + 1)
                            if s >= 2:
                                full_of(act, ("t", s - 2, 1))
                            act.activation(prob[:, s % 2, :], room(("s", s)), ACT.Exp, bias=negmax[:, s:s + 1], scale=-1.0,
                                           accum_out=rowsum[:, s:s + 1]).then_inc(free_sem(("s", s)), 1)
                        if 1 <= s <= SLOTS:
                            u, h = divmod(s - 1, 4)
                            full_of(act, ("t", s - 1, 1))
                            if u >= 2:
                                full_of(act, ("pv", u - 2))
                            act.activation(pt[:, u % 2, h, 4:8, :].rearrange("p k q -> p (k q)"), room(("t", s - 1, 1)),
                                           ACT.Copy).then_inc(free_sem(("t", s - 1, 1)), 1)
                        if s % 4 == 2 and s >= 6 and (s - 6) // 4 < UNITS:
                            u = (s - 6) // 4
                            full_of(act, ("pv", u))
                            act.activation(ots[:, u % 2, :], room(("pv", u))[:, 0:P], ACT.Copy).then_inc(free_sem(("pv", u)), 1)
                        if s % 4 == 0 and s >= 8:
                            u = (s - 8) // 4
                            full_of(act, ("ot", u))
                            act.activation(act_t[:, HI, u % 2, (u // 2) * P:(u // 2 + 1) * P], room(("ot", u))[:, 0:P],
                                           ACT.Copy).then_inc(ot_hi, 1)
                    deviation(2)
                    for blk in range(NBLK):
                        for k in range(KD):
                            to_tmp(("z2", blk, k), ACT.Identity, 512, scale=col["g2"][:, k:k + 1], bias=col["b2n"][:, k:k + 1])
                    for c in range(TT // 2):
                        for m in range(FM):
                            to_tmp(("w1", c, m), ACT.Gelu, 256, bias=col["b1"][:, m:m + 1])
                    for blk in range(NBLK):
                        for k in range(KD):
                            full_of(act, ("ht", blk, k))
                            act.activation(act_t[:, HI, k, blk * 512:(blk + 1) * 512], room(("ht", blk, k)),
                                           ACT.Copy).then_inc(ht_hi, 1)

                    def scale_agg(t, i):
                        act.wait_ge(w_ready, 2 * t + i + 1)
                        if t >= 1:
                            full_of(act, ("at", t - 1, i))
                        for e in range(2):
                            d = 2 * i + e
                            ins = act.activation(agg_s[:, d * D:(d + 1) * D], room(("agg", t, i))[:, 512 * e:512 * e + D],
                                                 ACT.Copy, scale=winv[:, t, d:d + 1])
                        ins.then_inc(free_sem(("agg", t, i)), 1)

                    def agg_high(t):
                        c = t // 2
                        for i in range(2):
                            full_of(act, ("at", t, i))
                            if c >= 1:
                                full_of(act, ("wd", c - 1, KD - 1))
                            act.activation(wide[:, HI, 4 * i:4 * i + 4, (t % 2) * P:(t % 2 + 1) * P],
                                           room(("at", t, i)).rearrange("p (k m) -> p k m", m=P), ACT.Copy).then_inc(agg_hi, 1)

                    def dense(c):
                        for m in range(KD):
                            to_tmp(("wd", c, m), ACT.Relu, 256, bias=col["bd"][:, m:m + 1])

                    def gru(t):
                        full_of(act, ("rz", t))
                        if t >= 2:
                            act.wait_ge(gru_out, t - 1)
                        act.activation(gates[:, t % 2, :], room(("rz", t)), ACT.Sigmoid).then_inc(free_sem(("rz", t)), 1)
                        free_of(act, ("n", t))
                        act.activation(cand[:, t % 2, :], tn[:, t % 2, :], ACT.Tanh).then_inc(tanh_done, 1)

                    for t in range(TT):
                        scale_agg(t, 0)
                        if t >= 1:
                            agg_high(t - 1)
                        scale_agg(t, 1)
                        if t >= 2 and t % 2 == 0:
                            dense(t // 2 - 1)
                        if t >= 3 and t % 2 == 1:
                            gru(t - 3)
                            gru(t - 2)
                    agg_high(TT - 1)
                    dense(TT // 2 - 1)
                    gru(TT - 2)
                    gru(TT - 1)
                    deviation(3)

                @block.vector
                def _(dve):
                    steps = [0]

                    def link(ins):
                        steps[0] += 1
                        ins.then_inc(dve_step, 1)
                        dve.wait_ge(dve_step, steps[0])

                    def moments(src, n):
                        for t in range(TT):
                            ins = dve.bn_stats(stats[:, t, :], src[:, t, :])
                        link(ins)
                        for t in range(TT):
                            ins = dve.bn_aggr(mv[:, t, :], stats[:, t, :])
                        ins.then_inc(ln_mv, 1)
                        dve.wait_ge(ln_sd, n)
                        link(dve.reciprocal(rstd[:, :], sd[:, :]))

                    def normalise(dst, src, t, signal):
                        dve.tensor_scalar(dst, src[:, t, :], mv[:, t, 0:1], rstd[:, t:t + 1], ALU.subtract,
                                          ALU.mult).then_inc(signal, 1)

                    def split(key, n, hi, lo):
                        j = splits[key]
                        free_of(dve, key)
                        link(dve.tensor_copy(hi, tmp[:, j % 2, 0:n]))
                        dve.tensor_tensor(lo, tmp[:, j % 2, 0:n], hi.bitcast(F32), ALU.subtract).then_inc(split_done, 1)

                    dve.wait_ge(x_in, 16)
                    moments(xin, 1)
                    for blk in range(NBLK):
                        if blk:
                            full_of(dve, ("z1", blk - 1, KD - 1))
                        for i in range(4):
                            normalise(z[:, i, :], xin, 4 * blk + i, z_ready)
                        for k in range(KD):
                            split(("z1", blk, k), 512, act_t[:, HI, k, blk * 512:(blk + 1) * 512],
                                  act_t[:, LO, k, blk * 512:(blk + 1) * 512])
                    for blk in range(NBLK):
                        for m in range(2 * KD):
                            split(("qk", blk, m), 512, qk_parts[:, blk, m, HI, :], qk_parts[:, blk, m, LO, :])

                    def score(s):
                        t = s // HEADS
                        full_of(dve, ("s", s))
                        dve.wait_ge(bias_ready, t + 1)
                        dve.tensor_tensor_reduce(room(("s", s)), room(("s", s)), bias[:, t % 2, :], -1.0, BIG, ALU.add,
                                                 ALU.min, negmax[:, s:s + 1]).then_inc(scored, 1)

                    def out_low(u):
                        dve.wait_ge(ot_hi, u + 1)
                        dve.tensor_tensor(act_t[:, LO, u % 2, (u // 2) * P:(u // 2 + 1) * P], room(("ot", u))[:, 0:P],
                                          act_t[:, HI, u % 2, (u // 2) * P:(u // 2 + 1) * P].bitcast(F32),
                                          ALU.subtract).then_inc(free_sem(("ot", u)), 1)

                    score(0)
                    score(1)
                    for s in range(SLOTS + 8):
                        if s + 2 < SLOTS:
                            score(s + 2)
                        if s < SLOTS:
                            u, h = divmod(s, 4)
                            full_of(dve, ("t", s, 0))
                            if u >= 2:
                                full_of(dve, ("pv", u - 2))
                            dve.tensor_copy(pt[:, u % 2, h, 0:4, :].rearrange("p k q -> p (k q)"),
                                            room(("t", s, 0))).then_inc(free_sem(("t", s, 0)), 1)
                        if s % 4 == 2 and s >= 6 and (s - 6) // 4 < UNITS:
                            u = (s - 6) // 4
                            free_of(dve, ("s", 4 * u + 3))
                            link(dve.reciprocal(rinv[:, 4 * u:4 * u + 4], rowsum[:, 4 * u:4 * u + 4]))
                            full_of(dve, ("otok", u))
                            dve.tensor_tensor(otok[:, u % 2, :, :], room(("otok", u))[:, 0:P].rearrange("p (h d) -> p h d", d=HD),
                                              rinv[:, 4 * u:4 * u + 4].rearrange("p (h a) -> p h a", a=1).broadcast_to([P, 4, HD]),
                                              ALU.mult).then_inc(free_sem(("otok", u)), 1)
                        if s % 4 == 0 and s >= 8:
                            out_low((s - 8) // 4)
                    for t in range(TT):
                        full_of(dve, ("wo", t))
                        dve.tensor_tensor(x1[:, t, :], room(("wo", t))[:, 0:D], xin[:, t, :], ALU.add).then_inc(free_sem(("wo", t)), 1)
                    free_of(dve, ("wo", TT - 2))
                    free_of(dve, ("wo", TT - 1))
                    moments(x1, 2)
                    for blk in range(NBLK):
                        if blk:
                            full_of(dve, ("z2", blk - 1, KD - 1))
                        for i in range(4):
                            normalise(z[:, i, :], x1, 4 * blk + i, z_ready)
                        for k in range(KD):
                            split(("z2", blk, k), 512, n2_t[:, HI, k, blk * 512:(blk + 1) * 512],
                                  n2_t[:, LO, k, blk * 512:(blk + 1) * 512])
                    for c in range(TT // 2):
                        for m in range(FM):
                            split(("w1", c, m), 256, wide[:, HI, m, :], wide[:, LO, m, :])
                        for t in (2 * c, 2 * c + 1):
                            full_of(dve, ("w2", t))
                            dve.tensor_tensor(x1[:, t, :], room(("w2", t))[:, 0:D], x1[:, t, :], ALU.add).then_inc(free_sem(("w2", t)), 1)
                    for blk in range(NBLK):
                        for k in range(KD):
                            dve.wait_ge(ht_hi, blk * KD + k + 1)
                            dve.tensor_tensor(act_t[:, LO, k, blk * 512:(blk + 1) * 512], room(("ht", blk, k)),
                                              act_t[:, HI, k, blk * 512:(blk + 1) * 512].bitcast(F32),
                                              ALU.subtract).then_inc(free_sem(("ht", blk, k)), 1)

                    def weight(t, i):
                        full_of(dve, ("agg", t, i))
                        counts = room(("agg", t, i)).rearrange("p (e n) -> p e n", e=2)[:, :, D]
                        w = winv[:, t, 2 * i:2 * i + 2]
                        link(dve.tensor_scalar(w, counts, AGG_EPS, None, ALU.add))
                        dve.reciprocal(w, w).then_inc(w_ready, 1)

                    def agg_low(t):
                        for i in range(2):
                            dve.wait_ge(agg_hi, 2 * t + i + 1)
                            dve.tensor_tensor(wide[:, LO, 4 * i:4 * i + 4, (t % 2) * P:(t % 2 + 1) * P],
                                              room(("at", t, i)).rearrange("p (k m) -> p k m", m=P),
                                              wide[:, HI, 4 * i:4 * i + 4, (t % 2) * P:(t % 2 + 1) * P].bitcast(F32),
                                              ALU.subtract).then_inc(free_sem(("at", t, i)), 1)

                    def dense(c):
                        for m in range(KD):
                            split(("wd", c, m), 256, out_t[:, HI, m, :], out_t[:, LO, m, :])

                    def gru(t):
                        free_of(dve, ("rz", t))
                        full_of(dve, ("n", t))
                        if t >= 2:
                            dve.wait_ge(gru_out, t - 1)
                        link(dve.tensor_tensor(tn[:, t % 2, :], room(("n", t))[:, D:2 * D], gates[:, t % 2, 0:D], ALU.mult))
                        dve.tensor_tensor(tn[:, t % 2, :], room(("n", t))[:, 0:D], tn[:, t % 2, :], ALU.add).then_inc(free_sem(("n", t)), 1)

                    for t in range(TT):
                        weight(t, 0)
                        if t >= 1:
                            agg_low(t - 1)
                        weight(t, 1)
                        if t >= 2 and t % 2 == 0:
                            dense(t // 2 - 1)
                        if t >= 3 and t % 2 == 1:
                            gru(t - 3)
                            gru(t - 2)
                    agg_low(TT - 1)
                    dense(TT // 2 - 1)
                    gru(TT - 2)
                    gru(TT - 1)
                    dve.wait_ge(gru_out, TT)
                    moments(x1, 3)
                    for t in range(TT):
                        normalise(x1[:, t, :], x1, t, z3_ready)

                @block.tensor
                def _(pe):
                    def mm3(dst, lhs, rhs, first, last):
                        pe.matmul(dst, lhs[HI], rhs[HI], start=first, stop=False)
                        pe.matmul(dst, lhs[HI], rhs[LO], start=False, stop=False)
                        return pe.matmul(dst, lhs[LO], rhs[HI], start=False, stop=last)

                    def parts(ap, *at):
                        return [ap[(slice(None), part) + at] for part in (HI, LO)]

                    def turn_rows(name, src, blk, ready):
                        for k in range(KD):
                            unit_clear(pe, (name, blk, k))
                        for i in range(4):
                            ready(i)
                            for k in range(KD):
                                ins = pe.transpose(room((name, blk, k))[:, i * P:(i + 1) * P], src(i)[:, k * P:(k + 1) * P], ident[:, :])
                                if i == 3:
                                    ins.then_inc(full_sem((name, blk, k)), 1)

                    for blk in range(NBLK):
                        turn_rows("z1", lambda i: z[:, i, :], blk, lambda i: pe.wait_ge(z_ready, 4 * blk + i + 1))
                    for blk in range(NBLK):
                        for m in range(2 * KD):
                            key = ("qk", blk, m)
                            unit_clear(pe, key)
                            w = w_at["qk"[m // KD]]
                            for k in range(KD):
                                pe.wait_ge(split_done, splits["z1", blk, k] + 1)
                                ins = mm3(room(key)[:, 0:512], parts(w, k, slice((m % KD) * P, (m % KD + 1) * P)),
                                          parts(act_t, k, slice(blk * 512, (blk + 1) * 512)), k == 0, k == KD - 1)
                            ins.then_inc(full_sem(key), 1)
                    for t in range(TT):
                        key = ("v", t)
                        unit_clear(pe, key)
                        pe.matmul(room(key)[:, 0:D], ones[0:2, :], row_v, start=True, stop=False)
                        for k in range(KD):
                            ins = mm3(room(key)[:, 0:D], parts(act_t, k, slice(t * P, (t + 1) * P)), parts(w_at["v"], k), False,
                                      k == KD - 1)
                        ins.then_inc(full_sem(key), 1)

                    def scores(s):
                        t, h = divmod(s, HEADS)
                        unit_clear(pe, ("s", s))
                        if s == 0:
                            pe.wait_ge(ks_in, 48)
                        if h == 0:
                            pe.wait_ge(qs_in[t % 2], 48 * (t // 2 + 1))
                        for i in range(2):
                            ins = pe.matmul(room(("s", s))[:, i * 512:(i + 1) * 512], qstack[:, t % 2, h, :],
                                            kstack[:, h, i * 512:(i + 1) * 512], start=True, stop=True)
                        ins.then_inc(full_sem(("s", s)), 1)

                    def turn_probs(s):
                        free_of(pe, ("s", s))
                        for i in range(2):
                            unit_clear(pe, ("t", s, i))
                            for k in range(4):
                                ins = pe.transpose(room(("t", s, i))[:, k * P:(k + 1) * P],
                                                   prob[:, s % 2, (4 * i + k) * P:(4 * i + k + 1) * P], ident[:, :])
                            ins.then_inc(full_sem(("t", s, i)), 1)

                    def attend(u):
                        g = u % 2
                        unit_clear(pe, ("pv", u))
                        free_of(pe, ("t", 4 * u + 3, 0))
                        free_of(pe, ("t", 4 * u + 3, 1))
                        if u == 0:
                            free_of(pe, ("v", TT - 2))
                            free_of(pe, ("v", TT - 1))
                        for k in range(TT):
                            for h in range(4):
                                ins = pe.matmul(room(("pv", u))[h * HD:(h + 1) * HD, 0:P],
                                                vtok[:, k, (4 * g + h) * HD:(4 * g + h + 1) * HD],
                                                pt[:, u % 2, h, k, :], start=(k == 0), stop=(k == TT - 1))
                        ins.then_inc(full_sem(("pv", u)), 1)

                    def turn_out(u):
                        unit_clear(pe, ("otok", u))
                        free_of(pe, ("pv", u))
                        pe.transpose(room(("otok", u))[:, 0:P], ots[:, u % 2, :], ident[:, :]).then_inc(full_sem(("otok", u)), 1)

                    def turn_back(u):
                        free_of(pe, ("otok", u))
                        pe.transpose(room(("ot", u))[:, 0:P], otok[:, u % 2, :, :].rearrange("p h d -> p (h d)"),
                                     ident[:, :]).then_inc(full_sem(("ot", u)), 1)

                    scores(0)
                    scores(1)
                    for s in range(SLOTS + 4):
                        if s + 2 < SLOTS:
                            scores(s + 2)
                        if s < SLOTS:
                            turn_probs(s)
                        if s % 4 == 0 and s >= 4:
                            attend(s // 4 - 1)
                        if s % 4 == 2 and s >= 6:
                            turn_out((s - 6) // 4)
                        if s % 4 == 3 and s >= 7:
                            turn_back((s - 7) // 4)

                    for t in range(TT):
                        key = ("wo", t)
                        unit_clear(pe, key)
                        free_of(pe, ("ot", 2 * t + 1))
                        pe.matmul(room(key)[:, 0:D], ones[32:34, :], row_o, start=True, stop=False)
                        for k in range(KD):
                            ins = mm3(room(key)[:, 0:D], parts(act_t, k, slice(t * P, (t + 1) * P)), parts(w_at["o"], k), False,
                                      k == KD - 1)
                        ins.then_inc(full_sem(key), 1)
                    for blk in range(NBLK):
                        turn_rows("z2", lambda i: z[:, i, :], blk, lambda i: pe.wait_ge(z_ready, TT + 4 * blk + i + 1))
                    for c in range(TT // 2):
                        for m in range(FM):
                            key = ("w1", c, m)
                            unit_clear(pe, key)
                            for k in range(KD):
                                pe.wait_ge(split_done, splits["z2", c // 2, k] + 1)
                                ins = mm3(room(key)[:, 0:256], parts(w_at["1"], k, slice(m * P, (m + 1) * P)),
                                          parts(n2_t, k, slice(c * 256, (c + 1) * 256)), k == 0, k == KD - 1)
                            ins.then_inc(full_sem(key), 1)
                        for t in (2 * c, 2 * c + 1):
                            key = ("w2", t)
                            unit_clear(pe, key)
                            pe.matmul(room(key)[:, 0:D], ones[32:34, :], row_2, start=True, stop=False)
                            for m in range(FM):
                                pe.wait_ge(split_done, splits["w1", c, m] + 1)
                                ins = mm3(room(key)[:, 0:D], parts(wide, m, slice((t % 2) * P, (t % 2 + 1) * P)),
                                          parts(w_at["2"], m), False, m == FM - 1)
                            ins.then_inc(full_sem(key), 1)
                    for blk in range(NBLK):
                        turn_rows("ht", lambda i: x1[:, 4 * blk + i, :], blk, lambda i: free_of(pe, ("w2", 4 * blk + i)))

                    def aggregate(t, i):
                        key = ("agg", t, i)
                        unit_clear(pe, key)
                        pe.wait_ge(hid_parts, TT)
                        for e in range(2):
                            d = 2 * i + e
                            pe.wait_ge(mask_ready, LABELS * t + d + 1)
                            for k in range(TT):
                                pe.matmul(room(key)[:, 512 * e:512 * e + D + 2], mask[:, d, k, :], hid_r[:, k, HI, :],
                                          start=(k == 0), stop=False)
                                ins = pe.matmul(room(key)[:, 512 * e:512 * e + D + 2], mask[:, d, k, :], hid_r[:, k, LO, :],
                                                start=False, stop=(k == TT - 1))
                        ins.then_inc(full_sem(key), 1)

                    def turn_agg(t):
                        for i in range(2):
                            unit_clear(pe, ("at", t, i))
                            free_of(pe, ("agg", t, i))
                            for k in range(4):
                                ins = pe.transpose(room(("at", t, i))[:, k * P:(k + 1) * P],
                                                   agg_s[:, (4 * i + k) * P:(4 * i + k + 1) * P], ident[:, :])
                            ins.then_inc(full_sem(("at", t, i)), 1)

                    def dense(c):
                        for m in range(KD):
                            key = ("wd", c, m)
                            unit_clear(pe, key)
                            pe.wait_ge(late_in, 32)
                            for i in range(2):
                                free_of(pe, ("at", 2 * c + 1, i))
                            for k in range(KA):
                                ins = mm3(room(key)[:, 0:256], parts(w_at["d"], k, slice(m * P, (m + 1) * P)),
                                          parts(wide, k), k == 0, k == KA - 1)
                            ins.then_inc(full_sem(key), 1)

                    def gru(t):
                        c, e = divmod(t, 2)
                        tok, half = slice(t * P, (t + 1) * P), slice(e * P, (e + 1) * P)
                        for k in range(KD):
                            pe.wait_ge(split_done, splits["wd", c, k] + 1)
                        for blk, k in ((t // 4, k) for k in range(KD)):
                            free_of(pe, ("ht", blk, k))
                        unit_clear(pe, ("rz", t))
                        dst = room(("rz", t))
                        pe.matmul(dst, ones[0:2, :], row_rz, start=True, stop=False)
                        for k in range(KD):
                            mm3(dst, parts(out_t, k, half), parts(w_at["rzi"], k), False, False)
                            ins = mm3(dst, parts(act_t, k, tok), parts(w_at["rzh"], k), False, k == KD - 1)
                        ins.then_inc(full_sem(("rz", t)), 1)
                        unit_clear(pe, ("n", t))
                        for at, row, src, w in ((0, row_ni, out_t, "ni"), (D, row_nh, act_t, "nh")):
                            dst = room(("n", t))[:, at:at + D]
                            pe.matmul(dst, ones[64:66, :], row, start=True, stop=False)
                            for k in range(KD):
                                ins = mm3(dst, parts(src, k, half if src is out_t else tok), parts(w_at[w], k), False, k == KD - 1)
                        ins.then_inc(full_sem(("n", t)), 1)

                    for t in range(TT):
                        aggregate(t, 0)
                        if t >= 1:
                            turn_agg(t - 1)
                        aggregate(t, 1)
                        if t >= 2 and t % 2 == 0:
                            dense(t // 2 - 1)
                        if t >= 3 and t % 2 == 1:
                            gru(t - 3)
                            gru(t - 2)
                    turn_agg(TT - 1)
                    dense(TT // 2 - 1)
                    gru(TT - 2)
                    gru(TT - 1)


def kernel(x, adj, L0_gnn_ln1_g, L0_gnn_ln1_b, L0_gnn_ln2_g, L0_gnn_ln2_b, L0_gnn_wq, L0_gnn_bq, L0_gnn_wk, L0_gnn_bk,
           L0_gnn_wv, L0_gnn_bv, L0_gnn_wo, L0_gnn_bo, L0_gnn_w1, L0_gnn_b1, L0_gnn_w2, L0_gnn_b2, L1_gnn_Wd, L1_gnn_bd,
           L1_gnn_Wri, L1_gnn_bri, L1_gnn_Wrh, L1_gnn_brh, L1_gnn_Wzi, L1_gnn_bzi, L1_gnn_Wzh, L1_gnn_bzh, L1_gnn_Wni,
           L1_gnn_bni, L1_gnn_Wnh, L1_gnn_bnh, L1_gnn_gamma, L1_gnn_beta):
    import concourse.bacc as bacc
    from concourse.bass_utils import run_bass_kernel_spmd

    turned = lambda w: np.ascontiguousarray(np.asarray(w).T)
    given = {
        "x": x, "adj": adj, "adj_t": np.ascontiguousarray(np.asarray(adj).transpose(0, 2, 1)),
        "ln1_g": L0_gnn_ln1_g, "ln1_b": L0_gnn_ln1_b, "ln2_g": L0_gnn_ln2_g, "ln2_b": L0_gnn_ln2_b,
        "wq": L0_gnn_wq, "bq": L0_gnn_bq, "wk": L0_gnn_wk, "bk": L0_gnn_bk, "wv": L0_gnn_wv, "bv": L0_gnn_bv,
        "wo": L0_gnn_wo, "bo": L0_gnn_bo, "w1": L0_gnn_w1, "b1": L0_gnn_b1, "w2": L0_gnn_w2, "b2": L0_gnn_b2,
        "wd_t": turned(L1_gnn_Wd), "bd": L1_gnn_bd,
        "wri_t": turned(L1_gnn_Wri), "bri": L1_gnn_bri, "wrh_t": turned(L1_gnn_Wrh), "brh": L1_gnn_brh,
        "wzi_t": turned(L1_gnn_Wzi), "bzi": L1_gnn_bzi, "wzh_t": turned(L1_gnn_Wzh), "bzh": L1_gnn_bzh,
        "wni_t": turned(L1_gnn_Wni), "bni": L1_gnn_bni, "wnh_t": turned(L1_gnn_Wnh), "bnh": L1_gnn_bnh,
        "gamma": L1_gnn_gamma, "beta": L1_gnn_beta,
    }
    nc = bacc.Bacc("TRN2", target_bir_lowering=False, num_devices=1)
    arrays, args = {}, []
    for name, a in given.items():
        a = np.ascontiguousarray(np.asarray(a))
        arrays[f"in_{name}"] = a
        args.append(nc.dram_tensor(f"in_{name}", a.shape, mybir.dt.from_np(a.dtype), kind="ExternalInput").ap())
    out = nc.dram_tensor("out_y", x.shape, F32, kind="ExternalOutput").ap()
    gated_graph_layers(nc, *args, out)
    r = run_bass_kernel_spmd(nc, [arrays], core_ids=[0])
    return r.results[0]["out_y"]
```

```python
from contextlib import ExitStack

import numpy as np

import concourse.bass as bass
from concourse import mybir

ALU = mybir.AluOpType
ACT = mybir.ActivationFunctionType
F32 = mybir.dt.float32
F32R = mybir.dt.float32r
I32 = mybir.dt.int32

P = 128
NEG = -1.0e30
BIG = 3.0e38
LN_EPS = 1e-5
ONE_LABEL = 0.2
AGG_EPS = 1e-8
HI, LO = 0, 1


class Plan:

    def __init__(self):
        self.place, self.uses, self.splits = {}, {}, {}

    def add(self, key, unit, split=False):
        self.uses[unit] = self.uses.get(unit, 0) + 1
        self.place[key] = (unit, self.uses[unit])
        if split:
            self.splits[key] = len(self.splits)

    def continued(self):
        other = Plan()
        other.place, other.uses, other.splits = dict(self.place), dict(self.uses), dict(self.splits)
        return other

    def use(self, full, free, unit_at):
        self.full, self.free, self.unit_at = full, free, unit_at

    def full_of(self, eng, key):
        unit, n = self.place[key]
        eng.wait_ge(self.full[unit], n)

    def free_of(self, eng, key):
        unit, n = self.place[key]
        eng.wait_ge(self.free[unit], n)

    def unit_clear(self, eng, key):
        unit, n = self.place[key]
        if n > 1:
            eng.wait_ge(self.free[unit], n - 1)

    def full_sem(self, key):
        return self.full[self.place[key][0]]

    def free_sem(self, key):
        return self.free[self.place[key][0]]

    def room(self, key):
        return self.unit_at[self.place[key][0]]


def gated_graph_layers(nc, x, adj, adj_t, ln1_g, ln1_b, ln2_g, ln2_b, wq, bq, wk, bk, wv, bv, wo, bo, w1, b1,
                       w2, b2, wd_t, bd, wri_t, bri, wrh_t, brh, wzi_t, bzi, wzh_t, bzh, wni_t, bni, wnh_t, bnh,
                       gamma, beta, out):
    NBATCH, S, D = x.shape
    HEADS = 8
    HD = D // HEADS
    TT = S // P
    KD = D // P
    NBLK = S // 512
    FF = w1.shape[1]
    FM = FF // P
    LABELS = wd_t.shape[0] // D
    KA = LABELS * KD
    SLOTS = TT * HEADS
    UNITS = SLOTS // 4
    ROWS = TT // 2 - 1
    QSCALE = float(1.0 / np.sqrt(HD))

    def plan_heads(plan):
        for blk in range(NBLK):
            for k in range(KD):
                plan.add(("z1", blk, k), f"T{k}", split=True)
        for which in "kq":
            for blk in range(NBLK):
                for m in range(KD):
                    plan.add((which, blk, m), f"R{m % 2}")
        for t in range(TT):
            plan.add(("v", t), "VM"[t % 2])

    def plan_first_layer(plan):
        for s in range(SLOTS):
            plan.add(("s", s), f"R{s % 2}")
            for i in range(2):
                plan.add(("t", s, i), f"T{i}")
        for u in range(UNITS):
            plan.add(("pv", u), "V")
            plan.add(("otok", u), "M")
            plan.add(("ot", u), "M")
            if u % 2:
                plan.add(("wo", u // 2), "M")
        for blk in range(NBLK):
            for k in range(KD):
                plan.add(("z2", blk, k), f"T{k}", split=True)
        for c in range(TT // 2):
            for m in range(FM):
                plan.add(("w1", c, m), f"R{m % 2}", split=True)
            for t in (2 * c, 2 * c + 1):
                plan.add(("w2", t), "VM"[t % 2])
            if c == 0:
                plan.add(("peak",), "T0")
        for blk in range(NBLK):
            for k in range(KD):
                plan.add(("ht", blk, k), f"T{k}")

    def plan_second_layer(plan, labels):
        for g in range(TT * labels // min(labels, 2)):
            plan.add(("agg", g), f"R{g % 2}")
            plan.add(("at", g), f"T{g % 2}")
        for c in range(TT // 2):
            for m in range(KD):
                plan.add(("wd", c, m), "VM"[m], split=True)
            for t in (2 * c, 2 * c + 1):
                plan.add(("rz", t), "V")
                plan.add(("n", t), "M")

    start, plan = Plan(), Plan()
    plan_heads(start)
    plan_first_layer(plan)
    every_label, one_label = plan.continued(), plan.continued()
    for second, labels in ((every_label, LABELS), (one_label, 1)):
        plan_second_layer(second, labels)
        plan_heads(second)

    ctx = ExitStack()
    with ctx:
        def sb(name, shape, dt):
            return ctx.enter_context(nc.sbuf_tensor(name, shape, dt))

        def sem(name):
            return ctx.enter_context(nc.semaphore(name))

        WP = 3 * KD * D + KD * D + KD * FF + FM * D
        weights = sb("weights", [P, 2, WP], F32R)
        LATE = KA * D + 2 * KD * 2 * D + 2 * KD * D
        shared_late = sb("late_or_stacks", [P, 2 * LATE], F32R)
        act_t = sb("act_t", [P, 2, KD, S], F32R)
        xin = sb("xin", [P, TT, D], F32)
        x1 = sb("x1", [P, TT, D], F32)
        z = sb("z", [P, 4, D], F32)
        tmp = sb("tmp", [P, 2, 512], F32)
        cols = sb("cols", [P, 24], F32)
        ident = sb("ident", [P, P], F32)
        ones = sb("ones", [P, P], F32R)
        rows = sb("rows", [P, 3 * D], F32R)
        gamma_b = sb("gamma_b", [P, D], F32)
        beta_b = sb("beta_b", [P, D], F32)
        stats = sb("stats", [P, TT, 6], F32)
        mv = sb("mv", [P, TT, 2], F32)
        var_eps = sb("var_eps", [P, TT], F32)
        mv1 = sb("mv1", [P, TT, 2], F32)
        var_eps1 = sb("var_eps1", [P, TT], F32)
        rstd1 = sb("rstd1", [P, TT], F32)
        peaks = sb("peaks", [P, TT], F32)
        peak = sb("peak", [P, 1], F32)
        many = sb("many", [1, 1], I32)
        rstd = sb("rstd", [P, TT], F32)
        minus_half = sb("minus_half", [P, TT], F32)
        negmax = sb("negmax", [P, SLOTS], F32)
        rowsum = sb("rowsum", [P, SLOTS], F32)
        rinv = sb("rinv", [P, SLOTS], F32)
        winv = sb("winv", [P, TT, LABELS], F32)
        adj_i = sb("adj_i", [P, 2, S], I32)
        edge = sb("edge", [P, LABELS * D], F32)
        with ExitStack() as a:
            pt = a.enter_context(nc.sbuf_tensor("pt", [P, 2, 4, TT, P], F32))
            bias = a.enter_context(nc.sbuf_tensor("bias", [P, 2, S], F32))
            vtok = a.enter_context(nc.sbuf_tensor("vtok", [P, TT, D], F32))
            prob = a.enter_context(nc.sbuf_tensor("prob", [P, 2, S], F32))
            ots = a.enter_context(nc.sbuf_tensor("ots", [P, 2, P], F32))
            otok = a.enter_context(nc.sbuf_tensor("otok", [P, 2, 4, HD], F32))
        with ExitStack() as a:
            qk_parts = a.enter_context(nc.sbuf_tensor("qk_parts", [P, 2, NBLK, KD, 2, 512], F32R))
        with ExitStack() as a:
            n2_mask = a.enter_context(nc.sbuf_tensor("n2_mask", [P, 4 * S], F32R))
            wide = a.enter_context(nc.sbuf_tensor("wide", [P, 2, 8, 256], F32R))
            hid_r = a.enter_context(nc.sbuf_tensor("hid_r", [P, TT, 2, D + 2], F32R))
            out_t = a.enter_context(nc.sbuf_tensor("out_t", [P, 2, KD, 256], F32R))
            tn = a.enter_context(nc.sbuf_tensor("tn", [P, 2, D], F32))
            gates = a.enter_context(nc.sbuf_tensor("gates", [P, 2, 2 * D], F32))
        ctx.enter_context(nc.sbuf_tensor("phase_area", [P, 14880], F32))

        psum = ctx.enter_context(nc.psum_tensor("psum", [P, 8 * 512], F32))
        unit_at = {"R0": psum[:, 0:1024], "R1": psum[:, 1024:2048], "T0": psum[:, 2048:2560],
                   "T1": psum[:, 2560:3072], "V": psum[:, 3072:3584], "M": psum[:, 3584:4096]}

        o = 0
        w_at = {}
        for name, k, n in (("q", KD, D), ("k", KD, D), ("v", KD, D), ("o", KD, D), ("1", KD, FF), ("2", FM, D)):
            w_at[name] = weights[:, :, o:o + k * n].rearrange("p h (k n) -> p h k n", k=k)
            o += k * n
        late = shared_late[:, :].rearrange("p (h n) -> p h n", h=2)
        o = 0
        for name, k, n in (("d", KA, D), ("rzi", KD, 2 * D), ("rzh", KD, 2 * D), ("ni", KD, D), ("nh", KD, D)):
            w_at[name] = late[:, :, o:o + k * n].rearrange("p h (k n) -> p h k n", k=k)
            o += k * n
        kstack = shared_late[0:3 * HD, 0:HEADS * S].rearrange("p (h s) -> p h s", h=HEADS)
        qstack = shared_late[0:3 * HD, HEADS * S:HEADS * S + 2 * HEADS * P].rearrange("p (r h q) -> p r h q", r=2, h=HEADS)
        n2_t = n2_mask[:, :].rearrange("p (h k s) -> p h k s", h=2, k=KD)
        mask = n2_mask[:, :].rearrange("p (r t m) -> p r t m", r=4, t=TT)
        agg_s = edge[:, :]
        col = {}
        for i, (name, k) in enumerate((("bq", KD), ("bk", KD), ("g1", KD), ("b1n", KD), ("g2", KD), ("b2n", KD),
                                       ("b1", FM), ("bd", KD))):
            at = sum(k_ for _, k_ in (("bq", KD), ("bk", KD), ("g1", KD), ("b1n", KD), ("g2", KD), ("b2n", KD),
                                      ("b1", FM), ("bd", KD))[:i])
            col[name] = cols[:, at:at + k]
        row_rz, row_v = rows[0:2, 0:2 * D], rows[0:2, 2 * D:3 * D]
        row_o, row_2 = rows[32:34, 0:D], rows[32:34, D:2 * D]
        row_ni, row_nh = rows[64:66, 0:D], rows[64:66, D:2 * D]

        late_d = nc.dram_tensor("late_weights", [P, 2, LATE], F32).ap()
        qk_d = nc.dram_tensor("qk_parts_d", [2, 2, D, S], F32).ap()

        full = {u: sem(f"full_{u}") for u in unit_at}
        free = {u: sem(f"free_{u}") for u in unit_at}
        x_in = sem("x_in")
        adj_in = [sem(f"adj_in{i}") for i in range(2)]
        stored = {w_: [sem(f"{w_}_stored{i}") for i in range(NBLK)] for w_ in "kq"}
        ks_in = sem("ks_in")
        qs_in = [sem(f"qs_in{i}") for i in range(2)]
        late_in = sem("late_in")
        y_out = sem("y_out")
        ln_mv = sem("ln_mv")
        ln_rstd = sem("ln_rstd")
        mv1_ready = sem("mv1_ready")
        rstd1_ready = sem("rstd1_ready")
        z1_ready = sem("z1_ready")
        z2_ready = sem("z2_ready")
        kq_hi = sem("kq_hi")
        edge_ready = sem("edge_ready")
        split_done = sem("split_done")
        dve_step = sem("dve_step")
        pool_step = sem("pool_step")
        bias_ready = sem("bias_ready")
        scored = sem("scored")
        ot_hi = sem("ot_hi")
        hid_parts = sem("hid_parts")
        ht_hi = sem("ht_hi")
        mask_ready = sem("mask_ready")
        w_ready = sem("w_ready")
        agg_hi = sem("agg_hi")
        tanh_done = sem("tanh_done")
        gru_out = sem("gru_out")
        z3_ready = sem("z3_ready")
        y_ready = sem("y_ready")
        batch_sems = [*full.values(), *free.values(), x_in, *adj_in, *stored["k"], *stored["q"], ks_in, *qs_in, late_in, y_out,
                      ln_mv, ln_rstd, mv1_ready, rstd1_ready, z1_ready, z2_ready, kq_hi, edge_ready, split_done, dve_step, pool_step, bias_ready, scored, ot_hi, hid_parts,
                      ht_hi, mask_ready, w_ready, agg_hi, tanh_done, gru_out, z3_ready, y_ready]
        many_known = sem("many_known")
        batch_sems.append(many_known)
        w_in = sem("w_in")
        w_in2 = sem("w_in2")
        w_split = sem("w_split")
        w_aux = sem("w_aux")
        rows_in = sem("rows_in")
        late_out = sem("late_out")
        w_ident = sem("w_ident")
        w_step = sem("w_step")

        for p_ in (start, plan, every_label, one_label):
            p_.use(full, free, unit_at)

        raw = pt[:, :, :, :, :].rearrange("p a b c d -> p (a b c d)")

        with nc.Block() as block:
            @block.sync
            def _(sp):
                o = 0
                for w, k, n in ((wq, KD, D), (wk, KD, D), (wv, KD, D), (wo, KD, D), (w1, KD, FF), (w2, FM, D)):
                    sp.dma_start(raw[:, o:o + k * n].rearrange("p (k n) -> p k n", k=k),
                                 w.rearrange("(k p) n -> p k n", p=P)).then_inc(w_in, 16)
                    o += k * n
                with nc.allow_non_contiguous_dma(reason="biases"):
                    for name, v in (("bq", bq), ("bk", bk), ("g1", ln1_g), ("b1n", ln1_b), ("g2", ln2_g),
                                    ("b2n", ln2_b), ("b1", b1), ("bd", bd)):
                        sp.dma_start(col[name], v.rearrange("(k p) -> p k", p=P)).then_inc(w_aux, 16)
                xrow = xin[0:1, :, :].rearrange("p t d -> p (t d)")
                x1row = x1[0:1, :, :].rearrange("p t d -> p (t d)")
                for i, v in enumerate((bri, bzi, bv, bo, b2, bni, bnh)):
                    sp.dma_start(x1row[:, i * D:(i + 1) * D], v.rearrange("(a n) -> a n", a=1)).then_inc(w_aux, 16)
                for i, v in enumerate((brh, bzh)):
                    sp.dma_start(xrow[:, i * D:(i + 1) * D], v.rearrange("(a n) -> a n", a=1)).then_inc(w_aux, 16)
                sp.dma_start(gamma_b[:, :], gamma.rearrange("(a n) -> a n", a=1).broadcast_to([P, D])).then_inc(w_aux, 16)
                sp.dma_start(beta_b[:, :], beta.rearrange("(a n) -> a n", a=1).broadcast_to([P, D])).then_inc(w_aux, 16)
                sp.wait_ge(w_split, 2)
                o = 0
                sp.dma_start(raw[:, 0:KA * D].rearrange("p (k n) -> p k n", k=KA),
                             wd_t.rearrange("(k p) n -> p k n", p=P)).then_inc(w_in2, 16)
                o = KA * D
                for pair in ((wri_t, wzi_t), (wrh_t, wzh_t), (wni_t,), (wnh_t,)):
                    n = len(pair) * D
                    dst = raw[:, o:o + KD * n].rearrange("p (k n) -> p k n", k=KD)
                    for i, w in enumerate(pair):
                        sp.dma_start(dst[:, :, i * D:(i + 1) * D], w.rearrange("(k p) n -> p k n", p=P)).then_inc(w_in2, 16)
                    o += KD * n
                sp.wait_ge(w_aux, 16 * 19 + 3)
                parts = act_t[0:1, :, :, :].rearrange("p h k s -> p h (k s)").bitcast(F32)
                for part in (HI, LO):
                    for base, at, a_, n in ((0, 0, 0, 3 * D), (32, 0, 3 * D, 2 * D), (64, 0, 5 * D, 2 * D)):
                        sp.dma_start(rows[base + part:base + part + 1, at:at + n].bitcast(F32),
                                     parts[:, part, a_:a_ + n]).then_inc(rows_in, 16)
                sp.wait_ge(w_split, 4)
                sp.dma_start(late_d, late.bitcast(F32)).then_inc(late_out, 16)
                sp.wait_ge(rows_in, 16 * 6)
                sp.wait_ge(late_out, 16)

            @block.vector
            def _(dve):
                dve.wait_ge(w_in, 16 * 6)
                dve.tensor_scalar(raw[:, 0:KD * D], raw[:, 0:KD * D], QSCALE, None, ALU.mult).then_inc(w_step, 1)
                dve.wait_ge(w_step, 1)
                dve.tensor_copy(weights[:, HI, :], raw[:, 0:WP]).then_inc(w_split, 1)
                dve.wait_ge(w_split, 1)
                dve.tensor_tensor(weights[:, LO, :], raw[:, 0:WP], weights[:, HI, :].bitcast(F32), ALU.subtract).then_inc(w_split, 1)
                dve.wait_ge(w_aux, 16 * 19)
                x1row = x1[0:1, :, :].rearrange("p t d -> p (t d)")
                xrow = xin[0:1, :, :].rearrange("p t d -> p (t d)")
                parts = act_t[0:1, :, :, :].rearrange("p h k s -> p h (k s)")
                dve.tensor_scalar(col["bq"], col["bq"], QSCALE, None, ALU.mult).then_inc(w_aux, 1)
                dve.wait_ge(w_aux, 16 * 19 + 1)
                dve.tensor_tensor(x1row[:, 0:2 * D], x1row[:, 0:2 * D], xrow[:, 0:2 * D], ALU.add).then_inc(w_aux, 1)
                dve.wait_ge(w_aux, 16 * 19 + 2)
                dve.tensor_copy(parts[:, HI, 0:7 * D], x1row[:, 0:7 * D]).then_inc(w_step, 1)
                dve.wait_ge(w_step, 2)
                dve.tensor_tensor(parts[:, LO, 0:7 * D], x1row[:, 0:7 * D], parts[:, HI, 0:7 * D].bitcast(F32),
                                  ALU.subtract).then_inc(w_aux, 1)
                dve.wait_ge(w_in2, 16 * 7)
                dve.tensor_copy(late[:, HI, :], raw[:, 0:LATE]).then_inc(w_split, 1)
                dve.wait_ge(w_split, 3)
                dve.tensor_tensor(late[:, LO, :], raw[:, 0:LATE], late[:, HI, :].bitcast(F32), ALU.subtract).then_inc(w_split, 1)

            @block.gpsimd
            def _(pool):
                pool.memset(ones[:, :].bitcast(F32), 1.0)
                pool.memset(minus_half[:, :], -0.5)
                pool.memset(ident[:, :], 0.0).then_inc(w_ident, 1)
                pool.wait_ge(w_ident, 1)
                pool.affine_select(out=ident[:, :], in_=ident[:, :], compare_op=ALU.not_equal, fill=1.0, base=0,
                                   pattern=[[-1, P]], channel_multiplier=1).then_inc(w_ident, 1)

        def rows_of(n):
            return adj[n].rearrange("(t p) k -> t p k", p=P)

        def load_x(sp, n):
            sp.dma_start(xin[:, :, :], x[n].rearrange("(t p) d -> p t d", p=P)).then_inc(x_in, 16)

        def load_queries(sp, t):
            for r, part in enumerate((HI, HI, LO)):
                sp.dma_start(qstack[r * HD:(r + 1) * HD, t % 2, :, :].bitcast(F32),
                             qk_d[0, part, :, t * P:(t + 1) * P].rearrange("(h d) s -> d h s", d=HD)).then_inc(qs_in[t % 2], 16)

        def sync_heads(sp, p, query_loads):
            def store_parts(i, which, blk):
                for m in range(KD):
                    p.free_of(sp, (which, blk, m))
                    dst = qk_d[i, :, m * P:(m + 1) * P, blk * 512:(blk + 1) * 512]
                    sp.dma_start(dst.rearrange("h p s -> p h s"),
                                 qk_parts[:, i, blk, m, :, :].bitcast(F32)).then_inc(stored[which][blk], 16)

            for blk in range(NBLK):
                store_parts(1, "k", blk)
            for blk in range(NBLK):
                sp.wait_ge(stored["k"][blk], 16 * KD)
                at = slice(blk * 512, (blk + 1) * 512)
                for r, part in enumerate((HI, LO, HI)):
                    sp.dma_start(kstack[r * HD:(r + 1) * HD, :, at].bitcast(F32),
                                 qk_d[1, part, :, at].rearrange("(h d) s -> d h s", d=HD)).then_inc(ks_in, 16)
            store_parts(0, "q", 0)
            sp.wait_ge(stored["q"][0], 16 * KD)
            load_queries(sp, 0)
            load_queries(sp, 1)
            store_parts(0, "q", 1)
            sp.wait_ge(stored["q"][1], 16 * KD)
            sp.wait_ge(ks_in, 48 * NBLK)
            for i in range(2):
                sp.wait_ge(qs_in[i], 48 * query_loads)

        def linker(eng, signal, steps):
            def link(ins):
                steps[0] += 1
                ins.then_inc(signal, 1)
                eng.wait_ge(signal, steps[0])

            return link

        def edge_square(dve, n, t, loads):
            dve.wait_ge(adj_in[t % 2], 16 * loads)
            if n >= 1:
                dve.wait_ge(bias_ready, n)
            dve.tensor_tensor_reduce(edge[:, :], adj_i[:, t % 2, :], adj_i[:, t % 2, :], 0.1, 0.0, ALU.mult, ALU.max,
                                     peaks[:, t:t + 1]).then_inc(edge_ready, 1)

        def edge_bias(pool, link, n, slot, loads):
            pool.wait_ge(adj_in[slot], 16 * loads)
            link(pool.tensor_scalar(bias[:, slot, :], adj_i[:, slot, :], 0.0, NEG, ALU.is_le, ALU.mult))
            pool.wait_ge(edge_ready, n + 1)
            pool.tensor_tensor(bias[:, slot, :], bias[:, slot, :], edge[:, :], ALU.add).then_inc(bias_ready, 1)

        def pool_deviation1(pool, link):
            pool.wait_ge(mv1_ready, 1)
            link(pool.tensor_scalar(var_eps1[:, :], mv1[:, :, 1], LN_EPS, None, ALU.add))
            pool.tensor_tensor(rstd1[:, :], var_eps1[:, :], minus_half[:, :], ALU.pow).then_inc(rstd1_ready, 1)

        def dve_moments1(dve, link):
            dve.wait_ge(x_in, 16)
            for t in range(TT):
                ins = dve.bn_stats(stats[:, t, :], xin[:, t, :])
            link(ins)
            for t in range(TT):
                ins = dve.bn_aggr(mv1[:, t, :], stats[:, t, :])
            ins.then_inc(mv1_ready, 1)

        def dve_normalise1(dve, p, blk):
            dve.wait_ge(rstd1_ready, 1)
            if blk:
                p.full_of(dve, ("z1", blk - 1, KD - 1))
            for i in range(4):
                t = 4 * blk + i
                dve.tensor_scalar(z[:, i, :], xin[:, t, :], mv1[:, t, 0:1], rstd1[:, t:t + 1], ALU.subtract,
                                  ALU.mult).then_inc(z1_ready, 1)

        def split(dve, p, link, key, n, hi, lo):
            j = p.splits[key]
            p.free_of(dve, key)
            link(dve.tensor_copy(hi, tmp[:, j % 2, 0:n]))
            dve.tensor_tensor(lo, tmp[:, j % 2, 0:n], hi.bitcast(F32), ALU.subtract).then_inc(split_done, 1)

        def dve_split1(dve, p, link, blk):
            for k in range(KD):
                split(dve, p, link, ("z1", blk, k), 512, act_t[:, HI, k, blk * 512:(blk + 1) * 512],
                      act_t[:, LO, k, blk * 512:(blk + 1) * 512])

        def dve_kq_low(dve, p, which):
            i = "qk".index(which)
            for blk in range(NBLK):
                for m in range(KD):
                    key = (which, blk, m)
                    dve.wait_ge(kq_hi, ("kq".index(which) * NBLK + blk) * KD + m + 1)
                    dve.scalar_tensor_tensor(qk_parts[:, i, blk, m, LO, :], p.room(key)[:, 0:512], col["b" + which][:, m:m + 1],
                                             qk_parts[:, i, blk, m, HI, :].bitcast(F32), ALU.add,
                                             ALU.subtract).then_inc(p.free_sem(key), 1)

        def to_tmp(act, p, key, func, n, **how):
            j = p.splits[key]
            if j >= 2:
                act.wait_ge(split_done, j - 1)
            p.full_of(act, key)
            act.activation(tmp[:, j % 2, 0:n], p.room(key)[:, 0:n], func, **how).then_inc(p.free_sem(key), 1)

        def act_affine1(act, p, blk):
            for k in range(KD):
                to_tmp(act, p, ("z1", blk, k), ACT.Identity, 512, scale=col["g1"][:, k:k + 1], bias=col["b1n"][:, k:k + 1])

        def act_heads(act, p):
            for i, which in ((1, "k"), (0, "q")):
                for blk in range(NBLK):
                    for m in range(KD):
                        key = (which, blk, m)
                        p.full_of(act, key)
                        act.activation(qk_parts[:, i, blk, m, HI, :], p.room(key)[:, 0:512], ACT.Identity,
                                       bias=col["b" + which][:, m:m + 1]).then_inc(kq_hi, 1)
            for t in range(TT):
                p.full_of(act, ("v", t))
                act.activation(vtok[:, t, :], p.room(("v", t))[:, 0:D], ACT.Copy).then_inc(p.free_sem(("v", t)), 1)

        def mm3(pe, dst, lhs, rhs, first, last):
            pe.matmul(dst, lhs[HI], rhs[HI], start=first, stop=False)
            pe.matmul(dst, lhs[HI], rhs[LO], start=False, stop=False)
            return pe.matmul(dst, lhs[LO], rhs[HI], start=False, stop=last)

        def parts(ap, *at):
            return [ap[(slice(None), part) + at] for part in (HI, LO)]

        def turn_rows(pe, p, name, src, blk, ready):
            for k in range(KD):
                p.unit_clear(pe, (name, blk, k))
            for i in range(4):
                ready(i)
                for k in range(KD):
                    ins = pe.transpose(p.room((name, blk, k))[:, i * P:(i + 1) * P], src(i)[:, k * P:(k + 1) * P], ident[:, :])
                    if i == 3:
                        ins.then_inc(p.full_sem((name, blk, k)), 1)

        def pe_turn1(pe, p, blk):
            turn_rows(pe, p, "z1", lambda i: z[:, i, :], blk, lambda i: pe.wait_ge(z1_ready, 4 * blk + i + 1))

        def pe_heads(pe, p):
            for key in [(w_, blk, m) for w_ in "kq" for blk in range(NBLK) for m in range(KD)]:
                which, blk, m = key
                p.unit_clear(pe, key)
                for k in range(KD):
                    pe.wait_ge(split_done, p.splits["z1", blk, k] + 1)
                    ins = mm3(pe, p.room(key)[:, 0:512], parts(w_at[which], k, slice(m * P, (m + 1) * P)),
                              parts(act_t, k, slice(blk * 512, (blk + 1) * 512)), k == 0, k == KD - 1)
                ins.then_inc(p.full_sem(key), 1)
            for t in range(TT):
                key = ("v", t)
                p.unit_clear(pe, key)
                pe.matmul(p.room(key)[:, 0:D], ones[0:2, :], row_v, start=True, stop=False)
                for k in range(KD):
                    ins = mm3(pe, p.room(key)[:, 0:D], parts(act_t, k, slice(t * P, (t + 1) * P)), parts(w_at["v"], k), False,
                              k == KD - 1)
                ins.then_inc(p.full_sem(key), 1)
            for t in (TT - 2, TT - 1):
                p.free_of(pe, ("v", t))

        def second_layer(p, NL, b_next, adjt_b, out_b, pool_steps, dve_steps):
            TOGETHER = min(NL, 2)
            GROUPS = NL // TOGETHER
            NK = TOGETHER * KD
            AHEAD = 1 if GROUPS == 2 else 2
            with nc.Block() as block:
                @block.sync
                def _(sp):
                    for t in range(2, TT):
                        sp.wait_ge(mask_ready, NL * (t - 1))
                        sp.dma_start(adj_i[:, t % 2, :].rearrange("p (n m) -> p n m", m=P), adjt_b[t]).then_inc(adj_in[t % 2], 16)
                    for i in range(2):
                        sp.wait_ge(mask_ready, NL * (TT - 1 + i))
                        sp.dma_start(adj_i[:, i, :], rows_of(b_next)[i]).then_inc(adj_in[i], 16)

                    def store_rows(t):
                        sp.wait_ge(y_ready, t + 1)
                        sp.dma_start(out_b[t], x1[:, t, :]).then_inc(y_out, 16)

                    for t in range(TT - 2):
                        store_rows(t)
                    sync_heads(sp, p, TT // 2)
                    for t in (TT - 2, TT - 1):
                        store_rows(t)
                    sp.wait_ge(y_out, 16 * TT)

                @block.gpsimd
                def _(pool):
                    link = linker(pool, pool_step, list(pool_steps))
                    norms = [NBLK]

                    def inverse_deviation(t0, n):
                        norms[0] += 1
                        pool.wait_ge(ln_mv, norms[0])
                        link(pool.tensor_scalar(var_eps[:, t0:t0 + n], mv[:, t0:t0 + n, 1], LN_EPS, None, ALU.add))
                        pool.tensor_tensor(rstd[:, t0:t0 + n], var_eps[:, t0:t0 + n], minus_half[:, 0:n], ALU.pow).then_inc(ln_rstd, 1)

                    def blend(t):
                        pool.wait_ge(tanh_done, t + 1)
                        diff = gates[:, t % 2, 0:D]
                        link(pool.tensor_tensor(diff, x1[:, t, :], tn[:, t % 2, :], ALU.subtract))
                        link(pool.tensor_tensor(diff, diff, gates[:, t % 2, D:2 * D], ALU.mult))
                        pool.tensor_tensor(x1[:, t, :], tn[:, t % 2, :], diff, ALU.add).then_inc(gru_out, 1)

                    def affine(t):
                        pool.wait_ge(z3_ready, t + 1)
                        link(pool.tensor_tensor(x1[:, t, :], x1[:, t, :], gamma_b[:, :], ALU.mult))
                        pool.tensor_tensor(x1[:, t, :], x1[:, t, :], beta_b[:, :], ALU.add).then_inc(y_ready, 1)

                    for t in range(TT):
                        blend(t)
                        if t % 2 == 0:
                            continue
                        inverse_deviation(t - 1, 2)
                        if t == TT - 1:
                            p.full_of(pool, ("agg", TT * GROUPS - 1))
                            edge_bias(pool, link, TT - 2, 0, ROWS + TT // 2 + 1)
                        affine(t - 1)
                        affine(t)
                        if t == 1:
                            pool_deviation1(pool, link)
                    edge_bias(pool, link, TT - 1, 1, ROWS + TT // 2 + 1)

                @block.scalar
                def _(act):
                    def scale_agg(t, i):
                        g = GROUPS * t + i
                        act.wait_ge(w_ready, g + 1)
                        if g >= 2:
                            p.full_of(act, ("at", g - 2))
                        for e in range(TOGETHER):
                            d, at = TOGETHER * i + e, g % 2 * 512 + e * D
                            ins = act.activation(agg_s[:, at:at + D], p.room(("agg", g))[:, 512 * e:512 * e + D],
                                                 ACT.Copy, scale=winv[:, t, d:d + 1])
                        ins.then_inc(p.free_sem(("agg", g)), 1)

                    def agg_high(t):
                        c = t // 2
                        for i in range(GROUPS):
                            p.full_of(act, ("at", GROUPS * t + i))
                            if c >= 1:
                                p.full_of(act, ("wd", c - 1, KD - 1))
                            act.activation(wide[:, HI, NK * i:NK * i + NK, (t % 2) * P:(t % 2 + 1) * P],
                                           p.room(("at", GROUPS * t + i))[:, 0:NK * P].rearrange("p (k m) -> p k m", m=P),
                                           ACT.Copy).then_inc(agg_hi, 1)

                    def dense(c):
                        for m in range(KD):
                            to_tmp(act, p, ("wd", c, m), ACT.Relu, 256, bias=col["bd"][:, m:m + 1])

                    def gru(t):
                        p.full_of(act, ("rz", t))
                        if t >= 2:
                            act.wait_ge(gru_out, t - 1)
                        act.activation(gates[:, t % 2, :], p.room(("rz", t)), ACT.Sigmoid).then_inc(p.free_sem(("rz", t)), 1)
                        p.free_of(act, ("n", t))
                        act.activation(tn[:, t % 2, :], tn[:, t % 2, :], ACT.Tanh).then_inc(tanh_done, 1)

                    for t in range(TT):
                        scale_agg(t, 0)
                        if t >= 1:
                            agg_high(t - 1)
                        if GROUPS == 2:
                            scale_agg(t, 1)
                        if t >= 2 and t % 2 == 0:
                            dense(t // 2 - 1)
                        if t >= 3 and t % 2 == 1:
                            gru(t - 3)
                            gru(t - 2)
                    agg_high(TT - 1)
                    dense(TT // 2 - 1)
                    act_affine1(act, p, 0)
                    gru(TT - 2)
                    gru(TT - 1)
                    act_affine1(act, p, 1)
                    act_heads(act, p)

                @block.vector
                def _(dve):
                    link = linker(dve, dve_step, list(dve_steps))
                    norms = [NBLK]

                    def moments(src, tiles):
                        for t in tiles:
                            ins = dve.bn_stats(stats[:, t, :], src[:, t, :])
                        link(ins)
                        for t in tiles:
                            ins = dve.bn_aggr(mv[:, t, :], stats[:, t, :])
                        ins.then_inc(ln_mv, 1)

                    def wait_for_deviation():
                        norms[0] += 1
                        dve.wait_ge(ln_rstd, norms[0])

                    def normalise(dst, src, t, signal):
                        dve.tensor_scalar(dst, src[:, t, :], mv[:, t, 0:1], rstd[:, t:t + 1], ALU.subtract,
                                          ALU.mult).then_inc(signal, 1)

                    def masks(t, labels):
                        if t >= TT:
                            return
                        dve.wait_ge(adj_in[t % 2], 16 * (ROWS + t // 2 + 1))
                        for d in labels:
                            n = NL * t + d
                            if n >= 4:
                                before, label = divmod(n - 4, NL)
                                p.full_of(dve, ("agg", GROUPS * before + label // TOGETHER))
                            dve.tensor_scalar(mask[:, n % 4, :, :], adj_i[:, t % 2, :].rearrange("p (n m) -> p n m", m=P),
                                              float(d + 1), None, ALU.is_equal).then_inc(mask_ready, 1)

                    def weight(t, i):
                        p.full_of(dve, ("agg", GROUPS * t + i))
                        counts = p.room(("agg", GROUPS * t + i)).rearrange("p (e n) -> p e n", e=2)[:, 0:TOGETHER, D]
                        w = winv[:, t, TOGETHER * i:TOGETHER * (i + 1)]
                        link(dve.tensor_scalar(w, counts, AGG_EPS, None, ALU.add))
                        dve.reciprocal(w, w).then_inc(w_ready, 1)

                    def agg_low(t):
                        for i in range(GROUPS):
                            g = GROUPS * t + i
                            at = (slice(NK * i, NK * (i + 1)), slice((t % 2) * P, (t % 2 + 1) * P))
                            dve.wait_ge(agg_hi, g + 1)
                            dve.tensor_tensor(wide[:, LO, at[0], at[1]],
                                              p.room(("at", g))[:, 0:NK * P].rearrange("p (k m) -> p k m", m=P),
                                              wide[:, HI, at[0], at[1]].bitcast(F32), ALU.subtract).then_inc(p.free_sem(("at", g)), 1)

                    def dense(c):
                        for m in range(KD):
                            split(dve, p, link, ("wd", c, m), 256, out_t[:, HI, m, :], out_t[:, LO, m, :])

                    def gru(t):
                        p.free_of(dve, ("rz", t))
                        p.full_of(dve, ("n", t))
                        if t >= 2:
                            dve.wait_ge(gru_out, t - 1)
                        link(dve.tensor_tensor(tn[:, t % 2, :], p.room(("n", t))[:, D:2 * D], gates[:, t % 2, 0:D], ALU.mult))
                        dve.tensor_tensor(tn[:, t % 2, :], p.room(("n", t))[:, 0:D], tn[:, t % 2, :], ALU.add).then_inc(p.free_sem(("n", t)), 1)

                    def last_moments(c):
                        dve.wait_ge(gru_out, 2 * c + 2)
                        moments(x1, (2 * c, 2 * c + 1))

                    def last_norm(c):
                        wait_for_deviation()
                        for t in (2 * c, 2 * c + 1):
                            normalise(x1[:, t, :], x1, t, z3_ready)

                    for t in range(AHEAD):
                        masks(t, range(NL))
                    for t in range(TT):
                        weight(t, 0)
                        if t >= 1:
                            agg_low(t - 1)
                        masks(t + AHEAD, range(TOGETHER))
                        if GROUPS == 2:
                            weight(t, 1)
                            masks(t + AHEAD, range(TOGETHER, NL))
                        if t >= 2 and t % 2 == 0:
                            dense(t // 2 - 1)
                        if t >= 3 and t % 2 == 1:
                            gru(t - 3)
                            gru(t - 2)
                        if t >= 4 and t % 2 == 0:
                            last_moments(t // 2 - 2)
                            last_norm(t // 2 - 2)
                        if t == 4:
                            dve_moments1(dve, link)
                        if t == 5:
                            dve_normalise1(dve, p, 0)
                    agg_low(TT - 1)
                    p.full_of(dve, ("at", TT * GROUPS - 1))
                    edge_square(dve, TT - 2, 0, ROWS + TT // 2 + 1)
                    dense(TT // 2 - 1)
                    last_moments(TT // 2 - 2)
                    dve_normalise1(dve, p, 1)
                    last_norm(TT // 2 - 2)
                    gru(TT - 2)
                    p.full_of(dve, ("n", TT - 1))
                    dve_split1(dve, p, link, 0)
                    gru(TT - 1)
                    dve_split1(dve, p, link, 1)
                    dve_kq_low(dve, p, "k")
                    last_moments(TT // 2 - 1)
                    dve_kq_low(dve, p, "q")
                    last_norm(TT // 2 - 1)
                    edge_square(dve, TT - 1, 1, ROWS + TT // 2 + 1)
                    dve.wait_ge(bias_ready, TT)

                @block.tensor
                def _(pe):
                    def aggregate(t, i):
                        key = ("agg", GROUPS * t + i)
                        p.unit_clear(pe, key)
                        pe.wait_ge(hid_parts, TT)
                        for e in range(TOGETHER):
                            n = NL * t + TOGETHER * i + e
                            pe.wait_ge(mask_ready, n + 1)
                            dst = p.room(key)[:, 512 * e:512 * e + D + 2]
                            for k in range(TT):
                                pe.matmul(dst, mask[:, n % 4, k, :], hid_r[:, k, HI, :], start=(k == 0), stop=False)
                                ins = pe.matmul(dst, mask[:, n % 4, k, :], hid_r[:, k, LO, :], start=False, stop=(k == TT - 1))
                        ins.then_inc(p.full_sem(key), 1)

                    def turn_agg(t):
                        for i in range(GROUPS):
                            g = GROUPS * t + i
                            p.unit_clear(pe, ("at", g))
                            p.free_of(pe, ("agg", g))
                            for k in range(NK):
                                at = g % 2 * 512 + k * P
                                ins = pe.transpose(p.room(("at", g))[:, k * P:(k + 1) * P], agg_s[:, at:at + P], ident[:, :])
                            ins.then_inc(p.full_sem(("at", g)), 1)

                    def dense(c):
                        for m in range(KD):
                            key = ("wd", c, m)
                            p.unit_clear(pe, key)
                            pe.wait_ge(late_in, 32)
                            for g in range(GROUPS * (2 * c + 1), GROUPS * (2 * c + 2)):
                                p.free_of(pe, ("at", g))
                            for k in range(NL * KD):
                                ins = mm3(pe, p.room(key)[:, 0:256], parts(w_at["d"], k, slice(m * P, (m + 1) * P)),
                                          parts(wide, k), k == 0, k == NL * KD - 1)
                            ins.then_inc(p.full_sem(key), 1)

                    def gru(t):
                        c, e = divmod(t, 2)
                        tok, half = slice(t * P, (t + 1) * P), slice(e * P, (e + 1) * P)
                        for k in range(KD):
                            pe.wait_ge(split_done, p.splits["wd", c, k] + 1)
                        for blk, k in ((t // 4, k) for k in range(KD)):
                            p.free_of(pe, ("ht", blk, k))
                        p.unit_clear(pe, ("rz", t))
                        dst = p.room(("rz", t))
                        pe.matmul(dst, ones[0:2, :], row_rz, start=True, stop=False)
                        for k in range(KD):
                            mm3(pe, dst, parts(out_t, k, half), parts(w_at["rzi"], k), False, False)
                            ins = mm3(pe, dst, parts(act_t, k, tok), parts(w_at["rzh"], k), False, k == KD - 1)
                        ins.then_inc(p.full_sem(("rz", t)), 1)
                        p.unit_clear(pe, ("n", t))
                        for at, row, src, w in ((0, row_ni, out_t, "ni"), (D, row_nh, act_t, "nh")):
                            dst = p.room(("n", t))[:, at:at + D]
                            pe.matmul(dst, ones[64:66, :], row, start=True, stop=False)
                            for k in range(KD):
                                ins = mm3(pe, dst, parts(src, k, half if src is out_t else tok), parts(w_at[w], k), False, k == KD - 1)
                        ins.then_inc(p.full_sem(("n", t)), 1)

                    for t in range(TT):
                        aggregate(t, 0)
                        if t >= 1:
                            turn_agg(t - 1)
                        if GROUPS == 2:
                            aggregate(t, 1)
                        if t >= 2 and t % 2 == 0:
                            dense(t // 2 - 1)
                        if t >= 3 and t % 2 == 1:
                            gru(t - 3)
                            gru(t - 2)
                    turn_agg(TT - 1)
                    dense(TT // 2 - 1)
                    pe_turn1(pe, p, 0)
                    gru(TT - 2)
                    gru(TT - 1)
                    pe_turn1(pe, p, 1)
                    pe_heads(pe, p)

        with nc.Block() as block:
            @block.sync
            def _(sp):
                load_x(sp, 0)
                for i in range(2):
                    sp.dma_start(adj_i[:, i, :], rows_of(0)[i]).then_inc(adj_in[i], 16)
                sync_heads(sp, start, 1)

            @block.gpsimd
            def _(pool):
                link = linker(pool, pool_step, [0])
                pool_deviation1(pool, link)
                for i in range(2):
                    edge_bias(pool, link, i, i, 1)

            @block.scalar
            def _(act):
                for blk in range(NBLK):
                    act_affine1(act, start, blk)
                act_heads(act, start)

            @block.vector
            def _(dve):
                link = linker(dve, dve_step, [0])
                dve_moments1(dve, link)
                dve_normalise1(dve, start, 0)
                dve_normalise1(dve, start, 1)
                dve_split1(dve, start, link, 0)
                edge_square(dve, 0, 0, 1)
                dve_split1(dve, start, link, 1)
                dve_kq_low(dve, start, "k")
                dve_kq_low(dve, start, "q")
                edge_square(dve, 1, 1, 1)
                dve.wait_ge(bias_ready, 2)

            @block.tensor
            def _(pe):
                for blk in range(NBLK):
                    pe_turn1(pe, start, blk)
                pe_heads(pe, start)

        with nc.Fori(0, NBATCH) as b:
            nc.all_engine_barrier()
            for s_ in batch_sems:
                nc.sync.sem_clear(s_)
            nc.all_engine_barrier()
            b_next = (b + 1) % NBATCH
            adj_b = rows_of(b)
            adjt_b = adj_t[b].rearrange("(n p) (t m) -> t p n m", p=P, m=P)
            out_b = out[b].rearrange("(t p) d -> t p d", p=P)
            pool_steps, dve_steps = [0], [0]
            with nc.Block() as block:

                @block.sync
                def _(sp):
                    for t in range(2, TT):
                        if t >= 4:
                            sp.wait_ge(bias_ready, t - 3)
                        sp.dma_start(adj_i[:, t % 2, :], adj_b[t]).then_inc(adj_in[t % 2], 16)
                        plan.full_of(sp, ("s", HEADS * (t - 1) - 1))
                        load_queries(sp, t)
                    for t in range(2):
                        sp.wait_ge(bias_ready, TT - 3 + t)
                        sp.dma_start(adj_i[:, t, :].rearrange("p (n m) -> p n m", m=P), adjt_b[t]).then_inc(adj_in[t], 16)
                    plan.full_of(sp, ("s", SLOTS - 1))
                    for part in (HI, LO):
                        sp.dma_start(late[:, part, :].bitcast(F32), late_d[:, part, :]).then_inc(late_in, 16)
                    plan.free_of(sp, ("wo", TT - 1))
                    load_x(sp, b_next)
                @block.gpsimd
                def _(pool):
                    link = linker(pool, pool_step, pool_steps)
                    norms = [0]

                    def inverse_deviation(t0, n):
                        norms[0] += 1
                        pool.wait_ge(ln_mv, norms[0])
                        link(pool.tensor_scalar(var_eps[:, t0:t0 + n], mv[:, t0:t0 + n, 1], LN_EPS, None, ALU.add))
                        pool.tensor_tensor(rstd[:, t0:t0 + n], var_eps[:, t0:t0 + n], minus_half[:, 0:n], ALU.pow).then_inc(ln_rstd, 1)

                    for t in range(2, TT):
                        pool.wait_ge(scored, HEADS * (t - 1))
                        edge_bias(pool, link, t - 2, t % 2, t // 2)
                    for blk in range(NBLK):
                        inverse_deviation(4 * blk, 4)

                    def hid_rows(t):
                        plan.free_of(pool, ("w2", t))
                        link(pool.tensor_copy(hid_r[:, t, HI, 0:D], x1[:, t, :]))
                        pool.tensor_tensor(hid_r[:, t, LO, 0:D], x1[:, t, :], hid_r[:, t, HI, 0:D].bitcast(F32),
                                           ALU.subtract).then_inc(hid_parts, 1)

                    plan.full_of(pool, ("w1", 0, FM - 1))
                    link(pool.memset(hid_r[:, :, :, D:D + 2].bitcast(F32), 0.0))
                    link(pool.memset(hid_r[:, :, HI, D:D + 1].bitcast(F32), 1.0))
                    for t in range(TT):
                        hid_rows(t)
                @block.scalar
                def _(act):
                    for s in range(SLOTS + 8):
                        if s < SLOTS:
                            act.wait_ge(scored, s + 1)
                            if s >= 2:
                                plan.full_of(act, ("t", s - 2, 1))
                            act.activation(prob[:, s % 2, :], plan.room(("s", s)), ACT.Exp, bias=negmax[:, s:s + 1], scale=-1.0,
                                           accum_out=rowsum[:, s:s + 1]).then_inc(plan.free_sem(("s", s)), 1)
                        if 1 <= s <= SLOTS:
                            u, h = divmod(s - 1, 4)
                            plan.full_of(act, ("t", s - 1, 1))
                            if u >= 2:
                                plan.full_of(act, ("pv", u - 2))
                            act.activation(pt[:, u % 2, h, 4:8, :].rearrange("p k q -> p (k q)"), plan.room(("t", s - 1, 1)),
                                           ACT.Copy).then_inc(plan.free_sem(("t", s - 1, 1)), 1)
                        if s % 4 == 3 and 7 <= s < SLOTS + 4:
                            u = (s - 7) // 4
                            plan.full_of(act, ("pv", u))
                            act.activation(ots[:, u % 2, :], plan.room(("pv", u))[:, 0:P], ACT.Copy).then_inc(plan.free_sem(("pv", u)), 1)
                        if s % 4 == 2 and s >= 10:
                            u = (s - 10) // 4
                            plan.full_of(act, ("ot", u))
                            act.activation(act_t[:, HI, u % 2, (u // 2) * P:(u // 2 + 1) * P], plan.room(("ot", u))[:, 0:P],
                                           ACT.Copy).then_inc(ot_hi, 1)
                    for blk in range(NBLK):
                        for k in range(KD):
                            to_tmp(act, plan, ("z2", blk, k), ACT.Identity, 512, scale=col["g2"][:, k:k + 1], bias=col["b2n"][:, k:k + 1])
                    for c in range(TT // 2):
                        for m in range(FM):
                            to_tmp(act, plan, ("w1", c, m), ACT.Gelu, 256, bias=col["b1"][:, m:m + 1])
                    for blk in range(NBLK):
                        for k in range(KD):
                            plan.full_of(act, ("ht", blk, k))
                            act.activation(act_t[:, HI, k, blk * 512:(blk + 1) * 512], plan.room(("ht", blk, k)),
                                           ACT.Copy).then_inc(ht_hi, 1)

                @block.vector
                def _(dve):
                    link = linker(dve, dve_step, dve_steps)
                    norms = [0]

                    def moments(src, tiles):
                        for t in tiles:
                            ins = dve.bn_stats(stats[:, t, :], src[:, t, :])
                        link(ins)
                        for t in tiles:
                            ins = dve.bn_aggr(mv[:, t, :], stats[:, t, :])
                        ins.then_inc(ln_mv, 1)

                    def wait_for_deviation():
                        norms[0] += 1
                        dve.wait_ge(ln_rstd, norms[0])

                    def normalise(dst, src, t, signal):
                        dve.tensor_scalar(dst, src[:, t, :], mv[:, t, 0:1], rstd[:, t:t + 1], ALU.subtract,
                                          ALU.mult).then_inc(signal, 1)

                    def residual(t):
                        plan.full_of(dve, ("wo", t))
                        dve.tensor_tensor(x1[:, t, :], plan.room(("wo", t))[:, 0:D], xin[:, t, :], ALU.add).then_inc(plan.free_sem(("wo", t)), 1)
                        plan.free_of(dve, ("wo", t))

                    def score(s):
                        t = s // HEADS
                        plan.full_of(dve, ("s", s))
                        if t >= 2:
                            dve.wait_ge(bias_ready, t - 1)
                        dve.tensor_tensor_reduce(plan.room(("s", s)), plan.room(("s", s)), bias[:, t % 2, :], -1.0, BIG, ALU.add,
                                                 ALU.min, negmax[:, s:s + 1]).then_inc(scored, 1)

                    def out_low(u):
                        dve.wait_ge(ot_hi, u + 1)
                        dve.tensor_tensor(act_t[:, LO, u % 2, (u // 2) * P:(u // 2 + 1) * P], plan.room(("ot", u))[:, 0:P],
                                          act_t[:, HI, u % 2, (u // 2) * P:(u // 2 + 1) * P].bitcast(F32),
                                          ALU.subtract).then_inc(plan.free_sem(("ot", u)), 1)

                    score(0)
                    score(1)
                    for s in range(SLOTS + 8):
                        if s + 2 < SLOTS:
                            score(s + 2)
                        if s < SLOTS:
                            u, h = divmod(s, 4)
                            plan.full_of(dve, ("t", s, 0))
                            if u >= 2:
                                plan.full_of(dve, ("pv", u - 2))
                            dve.tensor_copy(pt[:, u % 2, h, 0:4, :].rearrange("p k q -> p (k q)"),
                                            plan.room(("t", s, 0))).then_inc(plan.free_sem(("t", s, 0)), 1)
                        if s % 8 == 4 and s // 8 + 2 < TT:
                            t = s // 8 + 2
                            edge_square(dve, t - 2, t, t // 2)
                        if s % 8 == 0 and s >= 16:
                            residual(s // 8 - 2)
                            if s == 40:
                                moments(x1, range(4))
                        if s % 4 == 0 and s >= 8:
                            u = (s - 8) // 4
                            plan.free_of(dve, ("s", 4 * u + 3))
                            link(dve.reciprocal(rinv[:, 4 * u:4 * u + 4], rowsum[:, 4 * u:4 * u + 4]))
                            plan.full_of(dve, ("otok", u))
                            dve.tensor_tensor(otok[:, u % 2, :, :], plan.room(("otok", u))[:, 0:P].rearrange("p (h d) -> p h d", d=HD),
                                              rinv[:, 4 * u:4 * u + 4].rearrange("p (h a) -> p h a", a=1).broadcast_to([P, 4, HD]),
                                              ALU.mult).then_inc(plan.free_sem(("otok", u)), 1)
                        if s % 4 == 2 and s >= 10:
                            out_low((s - 10) // 4)
                    residual(TT - 1)
                    moments(x1, range(4, TT))
                    for blk in range(NBLK):
                        if blk:
                            plan.full_of(dve, ("z2", blk - 1, KD - 1))
                        wait_for_deviation()
                        for i in range(4):
                            normalise(z[:, i, :], x1, 4 * blk + i, z2_ready)
                        for k in range(KD):
                            split(dve, plan, link, ("z2", blk, k), 512, n2_t[:, HI, k, blk * 512:(blk + 1) * 512],
                                  n2_t[:, LO, k, blk * 512:(blk + 1) * 512])
                    dve.tensor_reduce(peak[:, :], peaks[:, :], mybir.AxisListType.X, ALU.max).then_inc(many_known, 1)
                    for c in range(TT // 2):
                        for m in range(FM):
                            split(dve, plan, link, ("w1", c, m), 256, wide[:, HI, m, :], wide[:, LO, m, :])
                        for t in (2 * c, 2 * c + 1):
                            plan.full_of(dve, ("w2", t))
                            dve.tensor_tensor(x1[:, t, :], plan.room(("w2", t))[:, 0:D], x1[:, t, :], ALU.add).then_inc(plan.free_sem(("w2", t)), 1)
                        if c == 0:
                            plan.full_of(dve, ("peak",))
                            dve.tensor_reduce(peak[0:1, :], plan.room(("peak",))[0:1, 0:P], mybir.AxisListType.X, ALU.max).then_inc(many_known, 1)
                            dve.wait_ge(many_known, 2)
                            dve.tensor_scalar(many[:, :], peak[0:1, :], ONE_LABEL, None, ALU.is_gt).then_inc(plan.free_sem(("peak",)), 1)
                            plan.free_of(dve, ("peak",))
                    for blk in range(NBLK):
                        for k in range(KD):
                            dve.wait_ge(ht_hi, blk * KD + k + 1)
                            dve.tensor_tensor(act_t[:, LO, k, blk * 512:(blk + 1) * 512], plan.room(("ht", blk, k)),
                                              act_t[:, HI, k, blk * 512:(blk + 1) * 512].bitcast(F32),
                                              ALU.subtract).then_inc(plan.free_sem(("ht", blk, k)), 1)

                @block.tensor
                def _(pe):
                    def scores(s):
                        t, h = divmod(s, HEADS)
                        plan.unit_clear(pe, ("s", s))
                        if h == 0 and t >= 2:
                            pe.wait_ge(qs_in[t % 2], 48 * (t // 2))
                        for i in range(2):
                            ins = pe.matmul(plan.room(("s", s))[:, i * 512:(i + 1) * 512], qstack[:, t % 2, h, :],
                                            kstack[:, h, i * 512:(i + 1) * 512], start=True, stop=True)
                        ins.then_inc(plan.full_sem(("s", s)), 1)

                    def turn_probs(s):
                        plan.free_of(pe, ("s", s))
                        for i in range(2):
                            plan.unit_clear(pe, ("t", s, i))
                            for k in range(4):
                                ins = pe.transpose(plan.room(("t", s, i))[:, k * P:(k + 1) * P],
                                                   prob[:, s % 2, (4 * i + k) * P:(4 * i + k + 1) * P], ident[:, :])
                            ins.then_inc(plan.full_sem(("t", s, i)), 1)

                    def attend(u, quarter):
                        g = u % 2
                        if quarter == 0:
                            plan.unit_clear(pe, ("pv", u))
                            plan.free_of(pe, ("t", 4 * u + 3, 0))
                            plan.free_of(pe, ("t", 4 * u + 3, 1))
                        for k in range(quarter * TT // 4, (quarter + 1) * TT // 4):
                            for h in range(4):
                                ins = pe.matmul(plan.room(("pv", u))[h * HD:(h + 1) * HD, 0:P],
                                                vtok[:, k, (4 * g + h) * HD:(4 * g + h + 1) * HD],
                                                pt[:, u % 2, h, k, :], start=(k == 0), stop=(k == TT - 1))
                        if quarter == 3:
                            ins.then_inc(plan.full_sem(("pv", u)), 1)

                    def turn_out(u):
                        plan.unit_clear(pe, ("otok", u))
                        plan.free_of(pe, ("pv", u))
                        pe.transpose(plan.room(("otok", u))[:, 0:P], ots[:, u % 2, :], ident[:, :]).then_inc(plan.full_sem(("otok", u)), 1)

                    def turn_back(u):
                        plan.free_of(pe, ("otok", u))
                        pe.transpose(plan.room(("ot", u))[:, 0:P], otok[:, u % 2, :, :].rearrange("p h d -> p (h d)"),
                                     ident[:, :]).then_inc(plan.full_sem(("ot", u)), 1)

                    def project(t):
                        key = ("wo", t)
                        plan.unit_clear(pe, key)
                        plan.free_of(pe, ("ot", 2 * t + 1))
                        pe.matmul(plan.room(key)[:, 0:D], ones[32:34, :], row_o, start=True, stop=False)
                        for k in range(KD):
                            ins = mm3(pe, plan.room(key)[:, 0:D], parts(act_t, k, slice(t * P, (t + 1) * P)), parts(w_at["o"], k), False,
                                      k == KD - 1)
                        ins.then_inc(plan.full_sem(key), 1)

                    scores(0)
                    scores(1)
                    for s in range(SLOTS + 8):
                        if 4 <= s < SLOTS + 4:
                            attend(s // 4 - 1, s % 4)
                        if s + 2 < SLOTS:
                            scores(s + 2)
                        if s < SLOTS:
                            turn_probs(s)
                        if s % 4 == 0 and s >= 8:
                            turn_out((s - 8) // 4)
                        if s % 4 == 1 and s >= 9:
                            turn_back((s - 9) // 4)
                        if s % 8 == 7 and s >= 15:
                            project((s - 15) // 8)
                    for blk in range(NBLK):
                        turn_rows(pe, plan, "z2", lambda i: z[:, i, :], blk, lambda i: pe.wait_ge(z2_ready, 4 * blk + i + 1))
                    for c in range(TT // 2):
                        for m in range(FM):
                            key = ("w1", c, m)
                            plan.unit_clear(pe, key)
                            for k in range(KD):
                                pe.wait_ge(split_done, plan.splits["z2", c // 2, k] + 1)
                                ins = mm3(pe, plan.room(key)[:, 0:256], parts(w_at["1"], k, slice(m * P, (m + 1) * P)),
                                          parts(n2_t, k, slice(c * 256, (c + 1) * 256)), k == 0, k == KD - 1)
                            ins.then_inc(plan.full_sem(key), 1)
                        for t in (2 * c, 2 * c + 1):
                            key = ("w2", t)
                            plan.unit_clear(pe, key)
                            pe.matmul(plan.room(key)[:, 0:D], ones[32:34, :], row_2, start=True, stop=False)
                            for m in range(FM):
                                pe.wait_ge(split_done, plan.splits["w1", c, m] + 1)
                                ins = mm3(pe, plan.room(key)[:, 0:D], parts(wide, m, slice((t % 2) * P, (t % 2 + 1) * P)),
                                          parts(w_at["2"], m), False, m == FM - 1)
                            ins.then_inc(plan.full_sem(key), 1)
                        if c == 0:
                            plan.unit_clear(pe, ("peak",))
                            pe.wait_ge(many_known, 1)
                            pe.transpose(plan.room(("peak",))[0:1, 0:P], peak[:, :], ident[:, :]).then_inc(plan.full_sem(("peak",)), 1)
                    for blk in range(NBLK):
                        turn_rows(pe, plan, "ht", lambda i: x1[:, 4 * blk + i, :], blk, lambda i: plan.free_of(pe, ("w2", 4 * blk + i)))

            has_many = nc.values_load(many[0:1, 0:1], min_val=0, max_val=1)
            with nc.If(has_many > 0):
                second_layer(every_label, LABELS, b_next, adjt_b, out_b, pool_steps, dve_steps)
            with nc.Else():
                second_layer(one_label, 1, b_next, adjt_b, out_b, pool_steps, dve_steps)


def kernel(x, adj, L0_gnn_ln1_g, L0_gnn_ln1_b, L0_gnn_ln2_g, L0_gnn_ln2_b, L0_gnn_wq, L0_gnn_bq, L0_gnn_wk, L0_gnn_bk,
           L0_gnn_wv, L0_gnn_bv, L0_gnn_wo, L0_gnn_bo, L0_gnn_w1, L0_gnn_b1, L0_gnn_w2, L0_gnn_b2, L1_gnn_Wd, L1_gnn_bd,
           L1_gnn_Wri, L1_gnn_bri, L1_gnn_Wrh, L1_gnn_brh, L1_gnn_Wzi, L1_gnn_bzi, L1_gnn_Wzh, L1_gnn_bzh, L1_gnn_Wni,
           L1_gnn_bni, L1_gnn_Wnh, L1_gnn_bnh, L1_gnn_gamma, L1_gnn_beta):
    import concourse.bacc as bacc
    from concourse.bass_utils import run_bass_kernel_spmd

    turned = lambda w: np.ascontiguousarray(np.asarray(w).T)
    given = {
        "x": x, "adj": adj, "adj_t": np.ascontiguousarray(np.asarray(adj).transpose(0, 2, 1)),
        "ln1_g": L0_gnn_ln1_g, "ln1_b": L0_gnn_ln1_b, "ln2_g": L0_gnn_ln2_g, "ln2_b": L0_gnn_ln2_b,
        "wq": L0_gnn_wq, "bq": L0_gnn_bq, "wk": L0_gnn_wk, "bk": L0_gnn_bk, "wv": L0_gnn_wv, "bv": L0_gnn_bv,
        "wo": L0_gnn_wo, "bo": L0_gnn_bo, "w1": L0_gnn_w1, "b1": L0_gnn_b1, "w2": L0_gnn_w2, "b2": L0_gnn_b2,
        "wd_t": turned(L1_gnn_Wd), "bd": L1_gnn_bd,
        "wri_t": turned(L1_gnn_Wri), "bri": L1_gnn_bri, "wrh_t": turned(L1_gnn_Wrh), "brh": L1_gnn_brh,
        "wzi_t": turned(L1_gnn_Wzi), "bzi": L1_gnn_bzi, "wzh_t": turned(L1_gnn_Wzh), "bzh": L1_gnn_bzh,
        "wni_t": turned(L1_gnn_Wni), "bni": L1_gnn_bni, "wnh_t": turned(L1_gnn_Wnh), "bnh": L1_gnn_bnh,
        "gamma": L1_gnn_gamma, "beta": L1_gnn_beta,
    }
    nc = bacc.Bacc("TRN2", target_bir_lowering=False, num_devices=1)
    arrays, args = {}, []
    for name, a in given.items():
        a = np.ascontiguousarray(np.asarray(a))
        arrays[f"in_{name}"] = a
        args.append(nc.dram_tensor(f"in_{name}", a.shape, mybir.dt.from_np(a.dtype), kind="ExternalInput").ap())
    out = nc.dram_tensor("out_y", x.shape, F32, kind="ExternalOutput").ap()
    gated_graph_layers(nc, *args, out)
    r = run_bass_kernel_spmd(nc, [arrays], core_ids=[0])
    return r.results[0]["out_y"]
```

```python
from contextlib import ExitStack

import numpy as np

import concourse.bass as bass
from concourse import mybir

ALU = mybir.AluOpType
ACT = mybir.ActivationFunctionType
F32 = mybir.dt.float32
F32R = mybir.dt.float32r
I32 = mybir.dt.int32

P = 128
NEG = -1.0e30
BIG = 3.0e38
LN_EPS = 1e-5
ONE_LABEL = 0.2
AGG_EPS = 1e-8
HI, LO = 0, 1


class Plan:

    def __init__(self):
        self.place, self.uses, self.splits = {}, {}, {}

    def add(self, key, unit, split=False):
        self.uses[unit] = self.uses.get(unit, 0) + 1
        self.place[key] = (unit, self.uses[unit])
        if split:
            self.splits[key] = len(self.splits)

    def continued(self):
        other = Plan()
        other.place, other.uses, other.splits = dict(self.place), dict(self.uses), dict(self.splits)
        return other

    def use(self, full, free, unit_at):
        self.full, self.free, self.unit_at = full, free, unit_at

    def full_of(self, eng, key):
        unit, n = self.place[key]
        eng.wait_ge(self.full[unit], n)

    def free_of(self, eng, key):
        unit, n = self.place[key]
        eng.wait_ge(self.free[unit], n)

    def unit_clear(self, eng, key):
        unit, n = self.place[key]
        if n > 1:
            eng.wait_ge(self.free[unit], n - 1)

    def full_sem(self, key):
        return self.full[self.place[key][0]]

    def free_sem(self, key):
        return self.free[self.place[key][0]]

    def room(self, key):
        return self.unit_at[self.place[key][0]]


def gated_graph_layers(nc, x, adj, adj_t, ln1_g, ln1_b, ln2_g, ln2_b, wq, bq, wk, bk, wv, bv, wo, bo, w1, b1,
                       w2, b2, wd_t, bd, wri_t, bri, wrh_t, brh, wzi_t, bzi, wzh_t, bzh, wni_t, bni, wnh_t, bnh,
                       gamma, beta, out):
    NBATCH, S, D = x.shape
    HEADS = 8
    HD = D // HEADS
    TT = S // P
    KD = D // P
    NBLK = S // 512
    FF = w1.shape[1]
    FM = FF // P
    LABELS = wd_t.shape[0] // D
    KA = LABELS * KD
    SLOTS = TT * HEADS
    UNITS = SLOTS // 4
    BY_SCALAR = (0, 4)
    EARLY = {SLOTS + 3: (0, 1), SLOTS + 4: (2,), SLOTS + 5: (3,), SLOTS + 6: (4, 5), SLOTS + 7: (6, 7)}
    assert NBLK == 2 and sorted(m for ms in EARLY.values() for m in ms) == list(range(FM))
    ROWS = (TT // 2 - 1, TT // 2)
    QSCALE = float(1.0 / np.sqrt(HD))

    KQ = [(which, blk, m) for blk in range(NBLK) for which in "kq" for m in range(KD)]

    def plan_heads(plan):
        for blk in range(NBLK):
            for k in range(KD):
                plan.add(("z1", blk, k), f"T{k}", split=True)
        for which, blk, m in KQ:
            plan.add((which, blk, m), f"R{m % 2}")
        for t in range(TT):
            plan.add(("v", t), "VM"[t % 2])

    def plan_first_layer(plan):
        for s in range(SLOTS):
            plan.add(("s", s), f"R{s % 2}")
            for i in range(2):
                plan.add(("t", s, i), f"T{i}")
        for u in range(UNITS):
            plan.add(("pv", u), "V")
            plan.add(("otok", u), "M")
            plan.add(("ot", u), "M")
            if u % 2:
                plan.add(("wo", u // 2), "M")
        for c in range(TT // 2):
            if c < NBLK:
                for k in range(KD):
                    plan.add(("z2", c, k), f"T{k}", split=True)
            for m in range(FM):
                plan.add(("w1", c, m), f"R{m % 2}", split=True)
            for t in (2 * c, 2 * c + 1):
                plan.add(("w2", t), "VM"[t % 2])
            if c == 1:
                plan.add(("peak",), "T0")
        for blk in range(NBLK):
            for k in range(KD):
                plan.add(("ht", blk, k), f"T{k}")

    def plan_second_layer(plan, labels):
        for g in range(TT * labels // min(labels, 2)):
            plan.add(("agg", g), f"R{g % 2}")
            plan.add(("at", g), f"T{g % 2}")
        for c in range(TT // 2):
            for m in range(KD):
                plan.add(("wd", c, m), "VM"[m], split=True)
            for t in (2 * c, 2 * c + 1):
                plan.add(("rz", t), "V")
                plan.add(("n", t), "M")

    start, plan = Plan(), Plan()
    plan_heads(start)
    plan_first_layer(plan)
    every_label, one_label = plan.continued(), plan.continued()
    for second, labels in ((every_label, LABELS), (one_label, 1)):
        plan_second_layer(second, labels)
        plan_heads(second)

    ctx = ExitStack()
    with ctx:
        def sb(name, shape, dt):
            return ctx.enter_context(nc.sbuf_tensor(name, shape, dt))

        def sem(name):
            return ctx.enter_context(nc.semaphore(name))

        WP = 3 * KD * D + KD * D + KD * FF + FM * D
        weights = sb("weights", [P, 2, WP], F32R)
        LATE = KA * D + 2 * KD * 2 * D + 2 * KD * D
        shared_late = sb("late_or_stacks", [P, 2 * LATE], F32R)
        act_t = sb("act_t", [P, 2, KD, S], F32R)
        xin = sb("xin", [P, TT, D], F32)
        x1 = sb("x1", [P, TT, D], F32)
        z = sb("z", [P, 4, D], F32)
        tmp = sb("tmp", [P, 2, 512], F32)
        cols = sb("cols", [P, 24], F32)
        ident = sb("ident", [P, P], F32)
        ones = sb("ones", [P, P], F32R)
        rows = sb("rows", [P, 3 * D], F32R)
        gamma_b = sb("gamma_b", [P, D], F32)
        beta_b = sb("beta_b", [P, D], F32)
        stats = sb("stats", [P, TT, 6], F32)
        mv = sb("mv", [P, TT, 2], F32)
        var_eps = sb("var_eps", [P, TT], F32)
        stats1 = sb("stats1", [P, TT, 6], F32)
        mv1 = sb("mv1", [P, TT, 2], F32)
        var_eps1 = sb("var_eps1", [P, TT], F32)
        rstd1 = sb("rstd1", [P, TT], F32)
        peaks = sb("peaks", [P, TT], F32)
        peak = sb("peak", [P, 1], F32)
        exp_ahead = sb("exp_ahead", [P, 1], F32)
        many = sb("many", [1, 1], I32)
        rstd = sb("rstd", [P, TT], F32)
        minus_half = sb("minus_half", [P, TT], F32)
        negmax = sb("negmax", [P, SLOTS], F32)
        rowsum = sb("rowsum", [P, SLOTS], F32)
        rinv = sb("rinv", [P, SLOTS], F32)
        winv = sb("winv", [P, TT, LABELS], F32)
        adj_i = sb("adj_i", [P, 2, S], I32)
        edge = sb("edge", [P, LABELS * D], F32)
        with ExitStack() as a:
            pt = a.enter_context(nc.sbuf_tensor("pt", [P, 2, 4, TT, P], F32))
            bias = a.enter_context(nc.sbuf_tensor("bias", [P, 2, S], F32))
            vtok = a.enter_context(nc.sbuf_tensor("vtok", [P, TT, D], F32))
            prob = a.enter_context(nc.sbuf_tensor("prob", [P, 2, S], F32))
            ots = a.enter_context(nc.sbuf_tensor("ots", [P, 2, P], F32))
            otok = a.enter_context(nc.sbuf_tensor("otok", [P, 2, 4, HD], F32))
        with ExitStack() as a:
            qk_parts = a.enter_context(nc.sbuf_tensor("qk_parts", [P, 2, NBLK, KD, 2, 512], F32R))
        with ExitStack() as a:
            raw = a.enter_context(nc.sbuf_tensor("raw", [P, WP + LATE], F32))
        with ExitStack() as a:
            n2_mask = a.enter_context(nc.sbuf_tensor("n2_mask", [P, 4 * S], F32R))
            wide = a.enter_context(nc.sbuf_tensor("wide", [P, 2, 8, 256], F32R))
            hid_r = a.enter_context(nc.sbuf_tensor("hid_r", [P, TT, 2, D + 2], F32R))
            out_t = a.enter_context(nc.sbuf_tensor("out_t", [P, 2, KD, 256], F32R))
            tn = a.enter_context(nc.sbuf_tensor("tn", [P, 2, D], F32))
            gates = a.enter_context(nc.sbuf_tensor("gates", [P, 2, 2 * D], F32))
        attention_size = 2 * 4 * TT * P + 2 * S + TT * D + 2 * S + 2 * P + 2 * 4 * HD
        second_size = 4 * S + 2 * 8 * 256 + TT * 2 * (D + 2) + 2 * KD * 256 + 2 * D + 2 * 2 * D
        ctx.enter_context(nc.sbuf_tensor("phase_area", [P, max(attention_size, second_size, WP + LATE)], F32))

        psum = ctx.enter_context(nc.psum_tensor("psum", [P, 8 * 512], F32))
        unit_at = {"R0": psum[:, 0:1024], "R1": psum[:, 1024:2048], "T0": psum[:, 2048:2560],
                   "T1": psum[:, 2560:3072], "V": psum[:, 3072:3584], "M": psum[:, 3584:4096]}

        o = 0
        w_at = {}
        for name, k, n in (("q", KD, D), ("k", KD, D), ("v", KD, D), ("o", KD, D), ("1", KD, FF), ("2", FM, D)):
            w_at[name] = weights[:, :, o:o + k * n].rearrange("p h (k n) -> p h k n", k=k)
            o += k * n
        late = shared_late[:, :].rearrange("p (h n) -> p h n", h=2)
        o = 0
        for name, k, n in (("d", KA, D), ("rzi", KD, 2 * D), ("rzh", KD, 2 * D), ("ni", KD, D), ("nh", KD, D)):
            w_at[name] = late[:, :, o:o + k * n].rearrange("p h (k n) -> p h k n", k=k)
            o += k * n
        kstack = shared_late[0:3 * HD, 0:HEADS * S].rearrange("p (h s) -> p h s", h=HEADS)
        qstack = shared_late[0:3 * HD, HEADS * S:HEADS * S + 2 * HEADS * P].rearrange("p (r h q) -> p r h q", r=2, h=HEADS)
        n2_t = n2_mask[:, :].rearrange("p (h k s) -> p h k s", h=2, k=KD)
        mask = n2_mask[:, :].rearrange("p (r t m) -> p r t m", r=4, t=TT)
        agg_s = edge[:, :]
        col = {}
        for i, (name, k) in enumerate((("bq", KD), ("bk", KD), ("g1", KD), ("b1n", KD), ("g2", KD), ("b2n", KD),
                                       ("b1", FM), ("bd", KD))):
            at = sum(k_ for _, k_ in (("bq", KD), ("bk", KD), ("g1", KD), ("b1n", KD), ("g2", KD), ("b2n", KD),
                                      ("b1", FM), ("bd", KD))[:i])
            col[name] = cols[:, at:at + k]
        row_rz, row_v = rows[0:2, 0:2 * D], rows[0:2, 2 * D:3 * D]
        row_o, row_2 = rows[32:34, 0:D], rows[32:34, D:2 * D]
        row_ni, row_nh = rows[64:66, 0:D], rows[64:66, D:2 * D]

        late_d = nc.dram_tensor("late_weights", [P, 2, LATE], F32).ap()
        q_d = nc.dram_tensor("q_parts", [2, D, S], F32).ap()

        full = {u: sem(f"full_{u}") for u in unit_at}
        free = {u: sem(f"free_{u}") for u in unit_at}
        x_in = sem("x_in")
        adj_in = [sem(f"adj_in{i}") for i in range(2)]
        late_in = sem("late_in")
        ln_mv = sem("ln_mv")
        ln_rstd = sem("ln_rstd")
        mv1_ready = sem("mv1_ready")
        rstd1_ready = sem("rstd1_ready")
        z1_ready = sem("z1_ready")
        z2_ready = sem("z2_ready")
        kq_hi = sem("kq_hi")
        edge_ready = sem("edge_ready")
        split_done = sem("split_done")
        dve_step = sem("dve_step")
        pool_step = sem("pool_step")
        bias_ready = sem("bias_ready")
        scored = sem("scored")
        ot_hi = sem("ot_hi")
        hid_parts = sem("hid_parts")
        ht_hi = sem("ht_hi")
        mask_ready = sem("mask_ready")
        w_ready = sem("w_ready")
        agg_hi = sem("agg_hi")
        tanh_done = sem("tanh_done")
        gru_out = sem("gru_out")
        z3_ready = sem("z3_ready")
        y_ready = sem("y_ready")
        batch_sems = [*full.values(), *free.values(), x_in, *adj_in, late_in,
                      ln_mv, ln_rstd, mv1_ready, rstd1_ready, z1_ready, z2_ready, kq_hi, edge_ready, split_done,
                      dve_step, pool_step, bias_ready, scored, ot_hi, hid_parts,
                      ht_hi, mask_ready, w_ready, agg_hi, tanh_done, gru_out, z3_ready, y_ready]
        many_known = sem("many_known")
        batch_sems.append(many_known)
        q_stored = [sem(f"q_stored{i}") for i in range(NBLK)]
        ks_in = sem("ks_in")
        qs_in = [sem(f"qs_in{i}") for i in range(2)]
        y_out = sem("y_out")
        carried_sems = [*q_stored, ks_in, *qs_in, y_out]
        K_LOADS = NBLK * (P // HD) * 3

        def span(sems):
            numbers = sorted(s_.num for s_ in sems)
            assert numbers == list(range(numbers[0], numbers[0] + len(sems)))
            return range(numbers[0], numbers[0] + len(sems))

        w_in = [sem(f"w_in{i}") for i in range(2)]
        w_hi = sem("w_hi")
        late_hi = sem("late_hi")
        affine_in = sem("affine_in")
        w_in2 = sem("w_in2")
        w_split = sem("w_split")
        w_aux = sem("w_aux")
        rows_in = sem("rows_in")
        late_out = sem("late_out")
        w_ident = sem("w_ident")
        w_step = sem("w_step")

        for p_ in (start, plan, every_label, one_label):
            p_.use(full, free, unit_at)


        def rows_of(n):
            return adj[n].rearrange("(t p) k -> t p k", p=P)

        def load_x(sp, n):
            sp.dma_start(xin[:, :, :], x[n].rearrange("(t p) d -> p t d", p=P)).then_inc(x_in, 16)

        def load_queries(sp, t):
            for r, part in enumerate((HI, HI, LO)):
                sp.dma_start(qstack[r * HD:(r + 1) * HD, t % 2, :, :].bitcast(F32),
                             q_d[part, :, t * P:(t + 1) * P].rearrange("(h d) s -> d h s", d=HD)).then_inc(qs_in[t % 2], 16)

        def store_queries(sp, blk):
            for m in range(KD):
                sp.dma_start(q_d[:, m * P:(m + 1) * P, blk * 512:(blk + 1) * 512].rearrange("h p s -> p h s"),
                             qk_parts[:, 0, blk, m, :, :].bitcast(F32)).then_inc(q_stored[blk], 16)

        def sync_heads(sp, p):
            k_heads = kstack.rearrange("p (m f) s -> p m f s", m=KD)
            for blk in range(NBLK):
                for m in range(KD):
                    p.free_of(sp, ("k", blk, m))
                for f in range(P // HD):
                    for r, part in enumerate((HI, LO, HI)):
                        sp.dma_start(k_heads[r * HD:(r + 1) * HD, :, f, blk * 512:(blk + 1) * 512].bitcast(F32),
                                     qk_parts[f * HD:(f + 1) * HD, 1, blk, :, part, :].bitcast(F32)).then_inc(ks_in, 16)
                if blk == 0:
                    for m in range(KD):
                        p.free_of(sp, ("q", blk, m))
                    store_queries(sp, blk)
            for m in range(KD):
                p.free_of(sp, ("q", NBLK - 1, m))
            sp.wait_ge(q_stored[0], 16 * KD)
            load_queries(sp, 0)
        def linker(eng, signal, steps):
            def link(ins):
                steps[0] += 1
                ins.then_inc(signal, 1)
                eng.wait_ge(signal, steps[0])

            return link

        def edge_square(dve, n, t, loads):
            dve.wait_ge(adj_in[t % 2], 16 * loads)
            if n >= 1:
                dve.wait_ge(bias_ready, n)
            dve.tensor_tensor_reduce(edge[:, :], adj_i[:, t % 2, :], adj_i[:, t % 2, :], 0.1, 0.0, ALU.mult, ALU.max,
                                     peaks[:, t:t + 1]).then_inc(edge_ready, 1)

        def edge_bias(pool, link, n, slot, loads):
            pool.wait_ge(adj_in[slot], 16 * loads)
            link(pool.tensor_scalar(bias[:, slot, :], adj_i[:, slot, :], 0.0, NEG, ALU.is_le, ALU.mult))
            pool.wait_ge(edge_ready, n + 1)
            pool.tensor_tensor(bias[:, slot, :], bias[:, slot, :], edge[:, :], ALU.add).then_inc(bias_ready, 1)

        def pool_deviation1(pool, link, moments):
            pool.wait_ge(mv1_ready, moments)
            link(pool.tensor_scalar(var_eps1[:, :], mv1[:, :, 1], LN_EPS, None, ALU.add))
            pool.tensor_tensor(rstd1[:, :], var_eps1[:, :], minus_half[:, :], ALU.pow).then_inc(rstd1_ready, 1)

        def dve_moments1(dve, link, tiles):
            dve.wait_ge(x_in, 16)
            for t in tiles:
                ins = dve.bn_stats(stats1[:, t, :], xin[:, t, :])
            link(ins)
            for t in tiles:
                ins = dve.bn_aggr(mv1[:, t, :], stats1[:, t, :])
            ins.then_inc(mv1_ready, 1)

        def dve_normalise1(dve, p, blk):
            dve.wait_ge(rstd1_ready, 1)
            if blk:
                p.full_of(dve, ("z1", blk - 1, KD - 1))
            for i in range(4):
                t = 4 * blk + i
                dve.tensor_scalar(z[:, i, :], xin[:, t, :], mv1[:, t, 0:1], rstd1[:, t:t + 1], ALU.subtract,
                                  ALU.mult).then_inc(z1_ready, 1)

        def split(dve, p, link, key, n, hi, lo):
            j = p.splits[key]
            p.free_of(dve, key)
            link(dve.tensor_copy(hi, tmp[:, j % 2, 0:n]))
            dve.tensor_tensor(lo, tmp[:, j % 2, 0:n], hi.bitcast(F32), ALU.subtract).then_inc(split_done, 1)

        def dve_split1(dve, p, link, blk):
            for k in range(KD):
                split(dve, p, link, ("z1", blk, k), 512, act_t[:, HI, k, blk * 512:(blk + 1) * 512],
                      act_t[:, LO, k, blk * 512:(blk + 1) * 512])

        def dve_kq_low(dve, p, blk):
            for key in KQ[len(KQ) // NBLK * blk:len(KQ) // NBLK * (blk + 1)]:
                which, _, m = key
                i = "qk".index(which)
                dve.wait_ge(kq_hi, KQ.index(key) + 1)
                dve.scalar_tensor_tensor(qk_parts[:, i, blk, m, LO, :], p.room(key)[:, 0:512], col["b" + which][:, m:m + 1],
                                         qk_parts[:, i, blk, m, HI, :].bitcast(F32), ALU.add,
                                         ALU.subtract).then_inc(p.free_sem(key), 1)

        def to_tmp(act, p, key, func, n, **how):
            j = p.splits[key]
            if j >= 2:
                act.wait_ge(split_done, j - 1)
            p.full_of(act, key)
            act.activation(tmp[:, j % 2, 0:n], p.room(key)[:, 0:n], func, **how).then_inc(p.free_sem(key), 1)

        def act_affine1(act, p, blk):
            for k in range(KD):
                to_tmp(act, p, ("z1", blk, k), ACT.Identity, 512, scale=col["g1"][:, k:k + 1], bias=col["b1n"][:, k:k + 1])

        def act_heads(act, p):
            for key in KQ:
                which, blk, m = key
                p.full_of(act, key)
                act.activation(qk_parts[:, "qk".index(which), blk, m, HI, :], p.room(key)[:, 0:512], ACT.Identity,
                               bias=col["b" + which][:, m:m + 1]).then_inc(kq_hi, 1)
            for t in range(TT):
                p.full_of(act, ("v", t))
                act.activation(vtok[:, t, :], p.room(("v", t))[:, 0:D], ACT.Copy).then_inc(p.free_sem(("v", t)), 1)

        def mm3(pe, dst, lhs, rhs, first, last):
            pe.matmul(dst, lhs[HI], rhs[HI], start=first, stop=False)
            pe.matmul(dst, lhs[HI], rhs[LO], start=False, stop=False)
            return pe.matmul(dst, lhs[LO], rhs[HI], start=False, stop=last)

        def parts(ap, *at):
            return [ap[(slice(None), part) + at] for part in (HI, LO)]

        def turn_rows(pe, p, name, src, blk, ready):
            for k in range(KD):
                p.unit_clear(pe, (name, blk, k))
            for i in range(4):
                ready(i)
                for k in range(KD):
                    ins = pe.transpose(p.room((name, blk, k))[:, i * P:(i + 1) * P], src(i)[:, k * P:(k + 1) * P], ident[:, :])
                    if i == 3:
                        ins.then_inc(p.full_sem((name, blk, k)), 1)

        def act_hid(act, p, blk):
            for k in range(KD):
                p.full_of(act, ("ht", blk, k))
                act.activation(act_t[:, HI, k, blk * 512:(blk + 1) * 512], p.room(("ht", blk, k)), ACT.Copy).then_inc(ht_hi, 1)

        def dve_hid(dve, p, blk):
            for k in range(KD):
                dve.wait_ge(ht_hi, blk * KD + k + 1)
                dve.tensor_tensor(act_t[:, LO, k, blk * 512:(blk + 1) * 512], p.room(("ht", blk, k)),
                                  act_t[:, HI, k, blk * 512:(blk + 1) * 512].bitcast(F32),
                                  ALU.subtract).then_inc(p.free_sem(("ht", blk, k)), 1)

        def pe_hid(pe, p, blk):
            turn_rows(pe, p, "ht", lambda i: x1[:, 4 * blk + i, :], blk, lambda i: p.free_of(pe, ("w2", 4 * blk + i)))

        def mask_of(dve, t, d, slot):
            dve.wait_ge(adj_in[t % 2], 16 * (ROWS[t % 2] + t // 2 + 1))
            dve.tensor_scalar(mask[:, slot, :, :], adj_i[:, t % 2, :].rearrange("p (n m) -> p n m", m=P),
                              float(d + 1), None, ALU.is_equal).then_inc(mask_ready, 1)

        def pe_turn1(pe, p, blk):
            turn_rows(pe, p, "z1", lambda i: z[:, i, :], blk, lambda i: pe.wait_ge(z1_ready, 4 * blk + i + 1))

        def pe_heads(pe, p):
            for key in KQ:
                which, blk, m = key
                p.unit_clear(pe, key)
                for k in range(KD):
                    pe.wait_ge(split_done, p.splits["z1", blk, k] + 1)
                    ins = mm3(pe, p.room(key)[:, 0:512], parts(w_at[which], k, slice(m * P, (m + 1) * P)),
                              parts(act_t, k, slice(blk * 512, (blk + 1) * 512)), k == 0, k == KD - 1)
                ins.then_inc(p.full_sem(key), 1)
            for t in range(TT):
                key = ("v", t)
                p.unit_clear(pe, key)
                pe.matmul(p.room(key)[:, 0:D], ones[0:2, :], row_v, start=True, stop=False)
                for k in range(KD):
                    ins = mm3(pe, p.room(key)[:, 0:D], parts(act_t, k, slice(t * P, (t + 1) * P)), parts(w_at["v"], k), False,
                              k == KD - 1)
                ins.then_inc(p.full_sem(key), 1)
            for t in (TT - 2, TT - 1):
                p.free_of(pe, ("v", t))

        def second_layer(p, NL, b_next, adjt_b, out_b, pool_steps, dve_steps):
            TOGETHER = min(NL, 2)
            GROUPS = NL // TOGETHER
            NK = TOGETHER * KD
            AHEAD = 1 if GROUPS == 2 else 2
            LATER = 0 if GROUPS == 2 else 1
            SETS = LABELS // NL
            with nc.Block() as block:
                @block.sync
                def _(sp):
                    for t in range(2, TT):
                        sp.wait_ge(mask_ready, NL * (t - 1))
                        sp.dma_start(adj_i[:, t % 2, :].rearrange("p (n m) -> p n m", m=P), adjt_b[t]).then_inc(adj_in[t % 2], 16)
                    sp.wait_ge(mask_ready, NL * (TT - 1))
                    sp.dma_start(adj_i[:, 0, :], rows_of(b_next)[0]).then_inc(adj_in[0], 16)

                    def store_rows(t):
                        sp.wait_ge(y_ready, t + 1)
                        sp.dma_start(out_b[t], x1[:, t, :]).then_inc(y_out, 16)

                    for t in range(TT - 2):
                        store_rows(t)
                    sync_heads(sp, p)
                    for t in (TT - 2, TT - 1):
                        store_rows(t)

                @block.gpsimd
                def _(pool):
                    link = linker(pool, pool_step, list(pool_steps))
                    norms = [NBLK]

                    def inverse_deviation(t0, n):
                        norms[0] += 1
                        pool.wait_ge(ln_mv, norms[0])
                        link(pool.tensor_scalar(var_eps[:, t0:t0 + n], mv[:, t0:t0 + n, 1], LN_EPS, None, ALU.add))
                        pool.tensor_tensor(rstd[:, t0:t0 + n], var_eps[:, t0:t0 + n], minus_half[:, 0:n], ALU.pow).then_inc(ln_rstd, 1)

                    def blend(t):
                        pool.wait_ge(tanh_done, t + 1)
                        diff = gates[:, t % 2, 0:D]
                        link(pool.tensor_tensor(diff, x1[:, t, :], tn[:, t % 2, :], ALU.subtract))
                        link(pool.tensor_tensor(diff, diff, gates[:, t % 2, D:2 * D], ALU.mult))
                        pool.tensor_tensor(x1[:, t, :], tn[:, t % 2, :], diff, ALU.add).then_inc(gru_out, 1)

                    def affine(t):
                        pool.wait_ge(z3_ready, t + 1)
                        link(pool.tensor_tensor(x1[:, t, :], x1[:, t, :], gamma_b[:, :], ALU.mult))
                        pool.tensor_tensor(x1[:, t, :], x1[:, t, :], beta_b[:, :], ALU.add).then_inc(y_ready, 1)

                    for t in range(TT):
                        blend(t)
                        if t % 2 == 0:
                            continue
                        inverse_deviation(t - 1, 2)
                        if t == TT - 3:
                            p.full_of(pool, ("agg", TT * GROUPS - 1))
                            edge_bias(pool, link, TT - 1, 0, ROWS[0] + TT // 2 + 1)
                        affine(t - 1)
                        affine(t)
                        if t == 1:
                            pool_deviation1(pool, link, TT // 2)

                @block.scalar
                def _(act):
                    def scale_agg(t, i):
                        g = GROUPS * t + i
                        act.wait_ge(w_ready, g + 1)
                        if g >= 2:
                            p.full_of(act, ("at", g - 2))
                        for e in range(TOGETHER):
                            d, at = TOGETHER * i + e, g % 2 * 512 + e * D
                            ins = act.activation(agg_s[:, at:at + D], p.room(("agg", g))[:, 512 * e:512 * e + D],
                                                 ACT.Copy, scale=winv[:, t, d:d + 1])
                        ins.then_inc(p.free_sem(("agg", g)), 1)

                    def agg_high(t):
                        c = t // 2
                        for i in range(GROUPS):
                            p.full_of(act, ("at", GROUPS * t + i))
                            if c >= SETS:
                                p.full_of(act, ("wd", c - SETS, KD - 1))
                            at = c % SETS * NL * KD + NK * i
                            act.activation(wide[:, HI, at:at + NK, (t % 2) * P:(t % 2 + 1) * P],
                                           p.room(("at", GROUPS * t + i))[:, 0:NK * P].rearrange("p (k m) -> p k m", m=P),
                                           ACT.Copy).then_inc(agg_hi, 1)

                    def dense(c):
                        for m in range(KD):
                            to_tmp(act, p, ("wd", c, m), ACT.Relu, 256, bias=col["bd"][:, m:m + 1])

                    def gru(t):
                        p.full_of(act, ("rz", t))
                        if t >= 2:
                            act.wait_ge(gru_out, t - 1)
                        act.activation(gates[:, t % 2, :], p.room(("rz", t)), ACT.Sigmoid).then_inc(p.free_sem(("rz", t)), 1)
                        p.free_of(act, ("n", t))
                        act.activation(tn[:, t % 2, :], tn[:, t % 2, :], ACT.Tanh).then_inc(tanh_done, 1)

                    act_hid(act, p, NBLK - 1)
                    for t in range(TT + LATER):
                        if t < TT:
                            scale_agg(t, 0)
                        if t >= 1:
                            agg_high(t - 1)
                        if GROUPS == 2:
                            scale_agg(t, 1)
                        pair, odd = divmod(t - LATER, 2)
                        if pair >= 1 and not odd:
                            dense(pair - 1)
                        if pair >= 1 and odd:
                            gru(2 * pair - 2)
                            gru(2 * pair - 1)
                    if not LATER:
                        agg_high(TT - 1)
                    dense(TT // 2 - 1)
                    act_affine1(act, p, 0)
                    gru(TT - 2)
                    gru(TT - 1)
                    act_affine1(act, p, 1)
                    act_heads(act, p)

                @block.vector
                def _(dve):
                    link = linker(dve, dve_step, list(dve_steps))
                    norms = [NBLK]

                    def moments(src, tiles):
                        for t in tiles:
                            ins = dve.bn_stats(stats[:, t, :], src[:, t, :])
                        link(ins)
                        for t in tiles:
                            ins = dve.bn_aggr(mv[:, t, :], stats[:, t, :])
                        ins.then_inc(ln_mv, 1)

                    def wait_for_deviation():
                        norms[0] += 1
                        dve.wait_ge(ln_rstd, norms[0])

                    def normalise(dst, src, t, signal):
                        dve.tensor_scalar(dst, src[:, t, :], mv[:, t, 0:1], rstd[:, t:t + 1], ALU.subtract,
                                          ALU.mult).then_inc(signal, 1)

                    def masks(t, labels):
                        for d in labels:
                            n = NL * t + d
                            if n >= 4:
                                before, label = divmod(n - 4, NL)
                                p.full_of(dve, ("agg", GROUPS * before + label // TOGETHER))
                            mask_of(dve, t, d, n % 4)

                    def weight(t, i):
                        p.full_of(dve, ("agg", GROUPS * t + i))
                        counts = p.room(("agg", GROUPS * t + i)).rearrange("p (e n) -> p e n", e=2)[:, 0:TOGETHER, D]
                        w = winv[:, t, TOGETHER * i:TOGETHER * (i + 1)]
                        link(dve.tensor_scalar(w, counts, AGG_EPS, None, ALU.add))
                        dve.reciprocal(w, w).then_inc(w_ready, 1)

                    def agg_low(t):
                        for i in range(GROUPS):
                            g = GROUPS * t + i
                            k = t // 2 % SETS * NL * KD + NK * i
                            at = (slice(k, k + NK), slice((t % 2) * P, (t % 2 + 1) * P))
                            dve.wait_ge(agg_hi, g + 1)
                            dve.tensor_tensor(wide[:, LO, at[0], at[1]],
                                              p.room(("at", g))[:, 0:NK * P].rearrange("p (k m) -> p k m", m=P),
                                              wide[:, HI, at[0], at[1]].bitcast(F32), ALU.subtract).then_inc(p.free_sem(("at", g)), 1)

                    def dense(c):
                        for m in range(KD):
                            split(dve, p, link, ("wd", c, m), 256, out_t[:, HI, m, :], out_t[:, LO, m, :])

                    def gru(t):
                        p.free_of(dve, ("rz", t))
                        p.full_of(dve, ("n", t))
                        if t >= 2:
                            dve.wait_ge(gru_out, t - 1)
                        link(dve.tensor_tensor(tn[:, t % 2, :], p.room(("n", t))[:, D:2 * D], gates[:, t % 2, 0:D], ALU.mult))
                        dve.tensor_tensor(tn[:, t % 2, :], p.room(("n", t))[:, 0:D], tn[:, t % 2, :], ALU.add).then_inc(p.free_sem(("n", t)), 1)

                    def last_moments(c):
                        dve.wait_ge(gru_out, 2 * c + 2)
                        moments(x1, (2 * c, 2 * c + 1))

                    def last_norm(c):
                        wait_for_deviation()
                        for t in (2 * c, 2 * c + 1):
                            normalise(x1[:, t, :], x1, t, z3_ready)

                    masks(0, range(1, NL))
                    for t in range(1, AHEAD):
                        masks(t, range(NL))
                    dve_hid(dve, p, NBLK - 1)
                    for t in range(TT + LATER):
                        if t < TT:
                            weight(t, 0)
                        if t >= 1:
                            agg_low(t - 1)
                        if t + AHEAD < TT:
                            masks(t + AHEAD, range(TOGETHER))
                        if GROUPS == 2:
                            weight(t, 1)
                            if t + AHEAD < TT:
                                masks(t + AHEAD, range(TOGETHER, NL))
                        pair, odd = divmod(t - LATER, 2)
                        if pair >= 1 and not odd:
                            dense(pair - 1)
                        if pair >= 1 and odd:
                            gru(2 * pair - 2)
                            gru(2 * pair - 1)
                        if pair >= 2 and not odd:
                            last_moments(pair - 2)
                            last_norm(pair - 2)
                        if 2 <= t < 2 + TT // 2:
                            dve_moments1(dve, link, (2 * t - 4, 2 * t - 3))
                        if t == 5 + LATER:
                            dve_normalise1(dve, p, 0)
                    if not LATER:
                        agg_low(TT - 1)
                    p.full_of(dve, ("at", TT * GROUPS - 1))
                    edge_square(dve, TT - 1, 0, ROWS[0] + TT // 2 + 1)
                    dense(TT // 2 - 1)
                    last_moments(TT // 2 - 2)
                    gru(TT - 2)
                    dve_normalise1(dve, p, 1)
                    p.full_of(dve, ("n", TT - 1))
                    dve_split1(dve, p, link, 0)
                    gru(TT - 1)
                    last_norm(TT // 2 - 2)
                    dve_split1(dve, p, link, 1)
                    dve_kq_low(dve, p, 0)
                    last_moments(TT // 2 - 1)
                    dve_kq_low(dve, p, 1)
                    last_norm(TT // 2 - 1)
                    dve.wait_ge(bias_ready, TT)

                @block.tensor
                def _(pe):
                    def aggregate(t, i):
                        key = ("agg", GROUPS * t + i)
                        p.unit_clear(pe, key)
                        for e in range(TOGETHER):
                            n = NL * t + TOGETHER * i + e
                            pe.wait_ge(mask_ready, n + 1)
                            dst = p.room(key)[:, 512 * e:512 * e + D + 2]
                            for k in range(TT):
                                if key == ("agg", 0) and e == 0:
                                    pe.wait_ge(hid_parts, k + 1)
                                pe.matmul(dst, mask[:, n % 4, k, :], hid_r[:, k, HI, :], start=(k == 0), stop=False)
                                ins = pe.matmul(dst, mask[:, n % 4, k, :], hid_r[:, k, LO, :], start=False, stop=(k == TT - 1))
                        ins.then_inc(p.full_sem(key), 1)

                    def turn_agg(t):
                        for i in range(GROUPS):
                            g = GROUPS * t + i
                            p.unit_clear(pe, ("at", g))
                            p.free_of(pe, ("agg", g))
                            for k in range(NK):
                                at = g % 2 * 512 + k * P
                                ins = pe.transpose(p.room(("at", g))[:, k * P:(k + 1) * P], agg_s[:, at:at + P], ident[:, :])
                            ins.then_inc(p.full_sem(("at", g)), 1)

                    def dense(c):
                        for m in range(KD):
                            key = ("wd", c, m)
                            p.unit_clear(pe, key)
                            pe.wait_ge(late_in, 32)
                            for g in range(GROUPS * (2 * c + 1), GROUPS * (2 * c + 2)):
                                p.free_of(pe, ("at", g))
                            for k in range(NL * KD):
                                ins = mm3(pe, p.room(key)[:, 0:256], parts(w_at["d"], k, slice(m * P, (m + 1) * P)),
                                          parts(wide, c % SETS * NL * KD + k), k == 0, k == NL * KD - 1)
                            ins.then_inc(p.full_sem(key), 1)

                    def gru(t):
                        c, e = divmod(t, 2)
                        tok, half = slice(t * P, (t + 1) * P), slice(e * P, (e + 1) * P)
                        for blk, k in ((t // 4, k) for k in range(KD)):
                            p.free_of(pe, ("ht", blk, k))
                        p.unit_clear(pe, ("rz", t))
                        dst = p.room(("rz", t))
                        pe.matmul(dst, ones[0:2, :], row_rz, start=True, stop=False)
                        for k in range(KD):
                            mm3(pe, dst, parts(act_t, k, tok), parts(w_at["rzh"], k), False, False)
                        for k in range(KD):
                            pe.wait_ge(split_done, p.splits["wd", c, k] + 1)
                            ins = mm3(pe, dst, parts(out_t, k, half), parts(w_at["rzi"], k), False, k == KD - 1)
                        ins.then_inc(p.full_sem(("rz", t)), 1)
                        p.unit_clear(pe, ("n", t))
                        for at, row, src, w in ((0, row_ni, out_t, "ni"), (D, row_nh, act_t, "nh")):
                            dst = p.room(("n", t))[:, at:at + D]
                            pe.matmul(dst, ones[64:66, :], row, start=True, stop=False)
                            for k in range(KD):
                                ins = mm3(pe, dst, parts(src, k, half if src is out_t else tok), parts(w_at[w], k), False, k == KD - 1)
                        ins.then_inc(p.full_sem(("n", t)), 1)

                    for t in range(TT + LATER):
                        if t < TT:
                            aggregate(t, 0)
                        if t == 0:
                            pe_hid(pe, p, NBLK - 1)
                        if t >= 1:
                            turn_agg(t - 1)
                        if GROUPS == 2:
                            aggregate(t, 1)
                        pair, odd = divmod(t - LATER, 2)
                        if pair >= 1 and not odd:
                            dense(pair - 1)
                        if pair >= 1 and odd:
                            gru(2 * pair - 2)
                            gru(2 * pair - 1)
                    if not LATER:
                        turn_agg(TT - 1)
                    dense(TT // 2 - 1)
                    pe_turn1(pe, p, 0)
                    gru(TT - 2)
                    gru(TT - 1)
                    pe_turn1(pe, p, 1)
                    pe_heads(pe, p)

        start_steps, start_pool_steps = [0], [0]
        raw_late = raw[:, WP:WP + LATE]
        NQKV = 3 * KD * D
        with nc.Block() as block:
            @block.sync
            def _(sp):
                load_x(sp, 0)
                o = 0
                for signal, ws in ((w_in[0], ((wq, KD, D), (wk, KD, D), (wv, KD, D))),
                                   (w_in[1], ((wo, KD, D), (w1, KD, FF), (w2, FM, D)))):
                    for w, k, n in ws:
                        sp.dma_start(raw[:, o:o + k * n].rearrange("p (k n) -> p k n", k=k),
                                     w.rearrange("(k p) n -> p k n", p=P)).then_inc(signal, 16)
                        o += k * n
                    if signal is w_in[1]:
                        continue
                    sp.dma_start(raw_late[:, 0:KA * D].rearrange("p (k n) -> p k n", k=KA),
                                 wd_t.rearrange("(k p) n -> p k n", p=P)).then_inc(w_in2, 16)
                    at = KA * D
                    for pair in ((wri_t, wzi_t), (wrh_t, wzh_t), (wni_t,), (wnh_t,)):
                        n = len(pair) * D
                        dst = raw_late[:, at:at + KD * n].rearrange("p (k n) -> p k n", k=KD)
                        for i, w in enumerate(pair):
                            sp.dma_start(dst[:, :, i * D:(i + 1) * D], w.rearrange("(k p) n -> p k n", p=P)).then_inc(w_in2, 16)
                        at += KD * n
                    with nc.allow_non_contiguous_dma(reason="biases"):
                        for name, v in (("bq", bq), ("bk", bk), ("g1", ln1_g), ("b1n", ln1_b), ("g2", ln2_g),
                                        ("b2n", ln2_b), ("b1", b1), ("bd", bd)):
                            sp.dma_start(col[name], v.rearrange("(k p) -> p k", p=P)).then_inc(w_aux, 16)
                    x1row = x1[0:1, :, :].rearrange("p t d -> p (t d)")
                    for i, v in enumerate((bri, bzi, bv, bo, b2, bni, bnh)):
                        sp.dma_start(x1row[:, i * D:(i + 1) * D], v.rearrange("(a n) -> a n", a=1)).then_inc(w_aux, 16)
                    for i, v in enumerate((brh, bzh)):
                        sp.dma_start(edge[0:1, i * D:(i + 1) * D], v.rearrange("(a n) -> a n", a=1)).then_inc(w_aux, 16)
                sp.dma_start(adj_i[:, 0, :], rows_of(0)[0]).then_inc(adj_in[0], 16)
                sp.dma_start(gamma_b[:, :], gamma.rearrange("(a n) -> a n", a=1).broadcast_to([P, D])).then_inc(affine_in, 16)
                sp.dma_start(beta_b[:, :], beta.rearrange("(a n) -> a n", a=1).broadcast_to([P, D])).then_inc(affine_in, 16)
                sp.wait_ge(w_aux, 16 * 17 + 3)
                bias_parts = act_t[0:1, :, :, :].rearrange("p h k s -> p h (k s)").bitcast(F32)
                for part in (HI, LO):
                    for base, at, a_, n in ((0, 0, 0, 3 * D), (32, 0, 3 * D, 2 * D), (64, 0, 5 * D, 2 * D)):
                        sp.dma_start(rows[base + part:base + part + 1, at:at + n].bitcast(F32),
                                     bias_parts[:, part, a_:a_ + n]).then_inc(rows_in, 16)
                for part in (HI, LO):
                    sp.wait_ge(late_hi if part == HI else w_split, 1 if part == HI else 2)
                    sp.dma_start(late_d[:, part, :], late[:, part, :].bitcast(F32)).then_inc(late_out, 16)
                sp.wait_ge(rows_in, 16 * 6)
                sp.wait_ge(affine_in, 32)

            @block.scalar
            def _(act):
                act.wait_ge(w_step, 1)
                act.activation(weights[:, HI, 0:NQKV], raw[:, 0:NQKV], ACT.Copy).then_inc(w_hi, 1)
                act.wait_ge(w_in2, 16 * 7)
                act.activation(late[:, HI, :], raw_late, ACT.Copy).then_inc(late_hi, 1)
                act.wait_ge(w_in[1], 16 * 3)
                act.activation(weights[:, HI, NQKV:WP], raw[:, NQKV:WP], ACT.Copy).then_inc(w_hi, 1)

            @block.vector
            def _(dve):
                link = linker(dve, dve_step, start_steps)
                dve_moments1(dve, link, range(TT))
                dve.wait_ge(w_in[0], 16 * 3)
                dve.tensor_scalar(raw[:, 0:KD * D], raw[:, 0:KD * D], QSCALE, None, ALU.mult).then_inc(w_step, 1)
                dve_normalise1(dve, start, 0)
                dve.wait_ge(w_hi, 1)
                dve.tensor_tensor(weights[:, LO, 0:NQKV], raw[:, 0:NQKV], weights[:, HI, 0:NQKV].bitcast(F32),
                                  ALU.subtract).then_inc(w_split, 1)
                dve.wait_ge(w_aux, 16 * 17)
                x1row = x1[0:1, :, :].rearrange("p t d -> p (t d)")
                bias_parts = act_t[0:1, :, :, :].rearrange("p h k s -> p h (k s)")
                dve.tensor_scalar(col["bq"], col["bq"], QSCALE, None, ALU.mult).then_inc(w_aux, 1)
                dve.wait_ge(w_aux, 16 * 17 + 1)
                dve.tensor_tensor(x1row[:, 0:2 * D], x1row[:, 0:2 * D], edge[0:1, 0:2 * D], ALU.add).then_inc(w_aux, 1)
                dve.wait_ge(w_aux, 16 * 17 + 2)
                dve.tensor_copy(bias_parts[:, HI, 0:7 * D], x1row[:, 0:7 * D]).then_inc(w_step, 1)
                dve.wait_ge(w_step, 2)
                dve.tensor_tensor(bias_parts[:, LO, 0:7 * D], x1row[:, 0:7 * D], bias_parts[:, HI, 0:7 * D].bitcast(F32),
                                  ALU.subtract).then_inc(w_aux, 1)
                dve.wait_ge(late_hi, 1)
                dve.tensor_tensor(late[:, LO, :], raw_late, late[:, HI, :].bitcast(F32), ALU.subtract).then_inc(w_split, 1)
                dve.wait_ge(w_hi, 2)
                dve.tensor_tensor(weights[:, LO, NQKV:WP], raw[:, NQKV:WP], weights[:, HI, NQKV:WP].bitcast(F32),
                                  ALU.subtract).then_inc(w_split, 1)

            @block.gpsimd
            def _(pool):
                pool.memset(ones[:, :].bitcast(F32), 1.0)
                pool.memset(ident[:, :], 0.0).then_inc(w_ident, 1)
                pool.memset(minus_half[:, :], -0.5).then_inc(w_ident, 1)
                pool.wait_ge(w_ident, 2)
                pool.affine_select(out=ident[:, :], in_=ident[:, :], compare_op=ALU.not_equal, fill=1.0, base=0,
                                   pattern=[[-1, P]], channel_multiplier=1).then_inc(w_ident, 1)
                pool_deviation1(pool, linker(pool, pool_step, start_pool_steps), 1)

        with nc.Block() as block:
            @block.sync
            def _(sp):
                sp.wait_ge(late_out, 32)
                sync_heads(sp, start)

            @block.gpsimd
            def _(pool):
                link = linker(pool, pool_step, start_pool_steps)
                edge_bias(pool, link, 0, 0, 1)

            @block.scalar
            def _(act):
                for blk in range(NBLK):
                    act_affine1(act, start, blk)
                act_heads(act, start)

            @block.vector
            def _(dve):
                link = linker(dve, dve_step, start_steps)
                dve_normalise1(dve, start, 1)
                dve_split1(dve, start, link, 0)
                edge_square(dve, 0, 0, 1)
                dve_split1(dve, start, link, 1)
                dve_kq_low(dve, start, 0)
                dve_kq_low(dve, start, 1)
                dve.wait_ge(bias_ready, 1)

            @block.tensor
            def _(pe):
                for blk in range(NBLK):
                    pe_turn1(pe, start, blk)
                pe_heads(pe, start)

        nc.sync.sem_inc(y_out, 16 * TT)
        with nc.Fori(0, NBATCH) as b:
            nc.sync.sem_clear(span(batch_sems))
            nc.all_engine_barrier()
            b_next = (b + 1) % NBATCH
            adj_b = rows_of(b)
            adjt_b = adj_t[b].rearrange("(n p) (t m) -> t p n m", p=P, m=P)
            out_b = out[b].rearrange("(t p) d -> t p d", p=P)
            pool_steps, dve_steps = [0], [0]
            with nc.Block() as block:

                @block.sync
                def _(sp):
                    store_queries(sp, 1)
                    sp.dma_start(adj_i[:, 1, :], adj_b[1]).then_inc(adj_in[1], 16)
                    load_queries(sp, 1)
                    for t in range(2, TT):
                        if t >= 3:
                            sp.wait_ge(bias_ready, t - 2)
                        sp.dma_start(adj_i[:, t % 2, :], adj_b[t]).then_inc(adj_in[t % 2], 16)
                        plan.full_of(sp, ("s", HEADS * (t - 1) - 1))
                        if t == 512 // P:
                            sp.wait_ge(q_stored[1], 16 * KD)
                        load_queries(sp, t)
                    for t in range(2):
                        sp.wait_ge(bias_ready, TT - 2 + t)
                        sp.dma_start(adj_i[:, t, :].rearrange("p (n m) -> p n m", m=P), adjt_b[t]).then_inc(adj_in[t], 16)
                    plan.full_of(sp, ("s", SLOTS - 1))
                    for part in (HI, LO):
                        sp.dma_start(late[:, part, :].bitcast(F32), late_d[:, part, :]).then_inc(late_in, 16)
                    plan.free_of(sp, ("wo", TT - 1))
                    load_x(sp, b_next)
                @block.gpsimd
                def _(pool):
                    link = linker(pool, pool_step, pool_steps)
                    norms = [0]

                    def inverse_deviation(t0, n):
                        norms[0] += 1
                        pool.wait_ge(ln_mv, norms[0])
                        link(pool.tensor_scalar(var_eps[:, t0:t0 + n], mv[:, t0:t0 + n, 1], LN_EPS, None, ALU.add))
                        pool.tensor_tensor(rstd[:, t0:t0 + n], var_eps[:, t0:t0 + n], minus_half[:, 0:n], ALU.pow).then_inc(ln_rstd, 1)

                    for t in range(1, TT):
                        if t >= 2:
                            pool.wait_ge(scored, HEADS * (t - 1))
                        edge_bias(pool, link, t - 1, t % 2, (t + 1) // 2)
                    for blk in range(NBLK):
                        inverse_deviation(4 * blk, 4)

                    def hid_rows(t):
                        plan.free_of(pool, ("w2", t))
                        link(pool.tensor_copy(hid_r[:, t, HI, 0:D], x1[:, t, :]))
                        pool.tensor_tensor(hid_r[:, t, LO, 0:D], x1[:, t, :], hid_r[:, t, HI, 0:D].bitcast(F32),
                                           ALU.subtract).then_inc(hid_parts, 1)

                    plan.full_of(pool, ("w1", 0, FM - 1))
                    link(pool.memset(hid_r[:, :, :, D:D + 2].bitcast(F32), 0.0))
                    link(pool.memset(hid_r[:, :, HI, D:D + 1].bitcast(F32), 1.0))
                    for t in range(TT):
                        hid_rows(t)
                @block.scalar
                def _(act):
                    act.activation(exp_ahead[:, :], ones[:, 0:1].bitcast(F32), ACT.Exp)

                    def affine2(blk):
                        for k in range(KD):
                            to_tmp(act, plan, ("z2", blk, k), ACT.Identity, 512, scale=col["g2"][:, k:k + 1], bias=col["b2n"][:, k:k + 1])

                    def gelu(c, m):
                        to_tmp(act, plan, ("w1", c, m), ACT.Gelu, 256, bias=col["b1"][:, m:m + 1])

                    for s in range(SLOTS + 8):
                        if s < SLOTS:
                            act.wait_ge(scored, s + 1)
                            if s >= 2:
                                plan.full_of(act, ("t", s - 2, 1))
                            act.activation(prob[:, s % 2, :], plan.room(("s", s)), ACT.Exp, bias=negmax[:, s:s + 1], scale=-1.0,
                                           accum_out=rowsum[:, s:s + 1]).then_inc(plan.free_sem(("s", s)), 1)
                        if 1 <= s <= SLOTS:
                            u, h = divmod(s - 1, 4)
                            if s - 1 == 2:
                                act.wait_ge(ks_in, 16 * K_LOADS)
                                act.wait_ge(q_stored[1], 16 * KD)
                            for i in ((0, 1) if (s - 1) % HEADS in BY_SCALAR else (1,)):
                                plan.full_of(act, ("t", s - 1, i))
                                if u >= 2:
                                    plan.full_of(act, ("pv", u - 2))
                                act.activation(pt[:, u % 2, h, 4 * i:4 * i + 4, :].rearrange("p k q -> p (k q)"),
                                               plan.room(("t", s - 1, i)), ACT.Copy).then_inc(plan.free_sem(("t", s - 1, i)), 1)
                        if s % 4 == 3 and 7 <= s < SLOTS + 4:
                            u = (s - 7) // 4
                            plan.full_of(act, ("pv", u))
                            act.activation(ots[:, u % 2, :], plan.room(("pv", u))[:, 0:P], ACT.Copy).then_inc(plan.free_sem(("pv", u)), 1)
                        if s % 4 == 2 and s >= 10:
                            u = (s - 10) // 4
                            plan.full_of(act, ("ot", u))
                            act.activation(act_t[:, HI, u % 2, (u // 2) * P:(u // 2 + 1) * P], plan.room(("ot", u))[:, 0:P],
                                           ACT.Copy).then_inc(ot_hi, 1)
                        if s == SLOTS:
                            affine2(0)
                        for m in EARLY.get(s, ()):
                            gelu(0, m)
                    affine2(1)
                    for c in range(1, TT // 2):
                        for m in range(FM):
                            gelu(c, m)
                        if c == 2:
                            act_hid(act, plan, 0)

                @block.vector
                def _(dve):
                    link = linker(dve, dve_step, dve_steps)
                    norms = [0]

                    def moments(src, tiles):
                        for t in tiles:
                            ins = dve.bn_stats(stats[:, t, :], src[:, t, :])
                        link(ins)
                        for t in tiles:
                            ins = dve.bn_aggr(mv[:, t, :], stats[:, t, :])
                        ins.then_inc(ln_mv, 1)

                    def wait_for_deviation():
                        norms[0] += 1
                        dve.wait_ge(ln_rstd, norms[0])

                    def normalise(dst, src, t, signal):
                        dve.tensor_scalar(dst, src[:, t, :], mv[:, t, 0:1], rstd[:, t:t + 1], ALU.subtract,
                                          ALU.mult).then_inc(signal, 1)

                    def residual(t):
                        plan.full_of(dve, ("wo", t))
                        if t == 0:
                            dve.wait_ge(y_out, 16 * TT)
                        dve.tensor_tensor(x1[:, t, :], plan.room(("wo", t))[:, 0:D], xin[:, t, :], ALU.add).then_inc(plan.free_sem(("wo", t)), 1)
                        plan.free_of(dve, ("wo", t))

                    def normalise2(blk):
                        if blk:
                            plan.full_of(dve, ("z2", blk - 1, KD - 1))
                        wait_for_deviation()
                        for i in range(4):
                            normalise(z[:, i, :], x1, 4 * blk + i, z2_ready)

                    def split2(blk):
                        for k in range(KD):
                            split(dve, plan, link, ("z2", blk, k), 512, n2_t[:, HI, k, blk * 512:(blk + 1) * 512],
                                  n2_t[:, LO, k, blk * 512:(blk + 1) * 512])

                    def split_gelu(c, m):
                        split(dve, plan, link, ("w1", c, m), 256, wide[:, HI, m, :], wide[:, LO, m, :])

                    def score(s):
                        t = s // HEADS
                        plan.full_of(dve, ("s", s))
                        if t >= 1:
                            dve.wait_ge(bias_ready, t)
                        dve.tensor_tensor_reduce(plan.room(("s", s)), plan.room(("s", s)), bias[:, t % 2, :], -1.0, BIG, ALU.add,
                                                 ALU.min, negmax[:, s:s + 1]).then_inc(scored, 1)

                    def out_low(u):
                        dve.wait_ge(ot_hi, u + 1)
                        dve.tensor_tensor(act_t[:, LO, u % 2, (u // 2) * P:(u // 2 + 1) * P], plan.room(("ot", u))[:, 0:P],
                                          act_t[:, HI, u % 2, (u // 2) * P:(u // 2 + 1) * P].bitcast(F32),
                                          ALU.subtract).then_inc(plan.free_sem(("ot", u)), 1)

                    score(0)
                    score(1)
                    for s in range(SLOTS + 8):
                        if s + 2 < SLOTS:
                            score(s + 2)
                        if s < SLOTS and s % HEADS not in BY_SCALAR:
                            u, h = divmod(s, 4)
                            if s == 2:
                                dve.wait_ge(ks_in, 16 * K_LOADS)
                                dve.wait_ge(q_stored[1], 16 * KD)
                            plan.full_of(dve, ("t", s, 0))
                            if u >= 2:
                                plan.full_of(dve, ("pv", u - 2))
                            dve.tensor_copy(pt[:, u % 2, h, 0:4, :].rearrange("p k q -> p (k q)"),
                                            plan.room(("t", s, 0))).then_inc(plan.free_sem(("t", s, 0)), 1)
                        if s == 0:
                            edge_square(dve, 0, 1, 1)
                        if s % 8 == 4 and s // 8 + 2 < TT:
                            t = s // 8 + 2
                            edge_square(dve, t - 1, t, (t + 1) // 2)
                        if s % 8 == 0 and s >= 16:
                            residual(s // 8 - 2)
                            if s == 40:
                                moments(x1, range(4))
                        if s % 4 == 0 and s >= 8:
                            u = (s - 8) // 4
                            plan.free_of(dve, ("s", 4 * u + 3))
                            link(dve.reciprocal(rinv[:, 4 * u:4 * u + 4], rowsum[:, 4 * u:4 * u + 4]))
                            plan.full_of(dve, ("otok", u))
                            dve.tensor_tensor(otok[:, u % 2, :, :], plan.room(("otok", u))[:, 0:P].rearrange("p (h d) -> p h d", d=HD),
                                              rinv[:, 4 * u:4 * u + 4].rearrange("p (h a) -> p h a", a=1).broadcast_to([P, 4, HD]),
                                              ALU.mult).then_inc(plan.free_sem(("otok", u)), 1)
                        if s % 4 == 2 and s >= 10:
                            out_low((s - 10) // 4)
                        if s == SLOTS - 6:
                            normalise2(0)
                        if s == SLOTS:
                            plan.full_of(dve, ("pv", UNITS - 2))
                            split2(0)
                        for m in EARLY.get(s, ()):
                            split_gelu(0, m)
                    residual(TT - 1)
                    moments(x1, range(4, TT))
                    dve.tensor_reduce(peak[:, :], peaks[:, :], mybir.AxisListType.X, ALU.max).then_inc(many_known, 1)
                    for c in range(TT // 2):
                        if c == 1:
                            split2(1)
                        if c >= 1:
                            for m in range(FM):
                                split_gelu(c, m)
                        if c == 0:
                            normalise2(1)
                        if c == TT // 2 - 1:
                            plan.full_of(dve, ("w1", c, FM - 1))
                            mask_of(dve, 0, 0, 0)
                        for t in (2 * c, 2 * c + 1):
                            plan.full_of(dve, ("w2", t))
                            dve.tensor_tensor(x1[:, t, :], plan.room(("w2", t))[:, 0:D], x1[:, t, :], ALU.add).then_inc(plan.free_sem(("w2", t)), 1)
                        if c == 1:
                            plan.full_of(dve, ("peak",))
                            dve.tensor_reduce(peak[0:1, :], plan.room(("peak",))[0:1, 0:P], mybir.AxisListType.X, ALU.max).then_inc(many_known, 1)
                            dve.wait_ge(many_known, 2)
                            dve.tensor_scalar(many[:, :], peak[0:1, :], ONE_LABEL, None, ALU.is_gt).then_inc(plan.free_sem(("peak",)), 1)
                            plan.free_of(dve, ("peak",))
                        if c == 2:
                            dve_hid(dve, plan, 0)

                @block.tensor
                def _(pe):
                    def scores(s):
                        t, h = divmod(s, HEADS)
                        plan.unit_clear(pe, ("s", s))
                        if s == 0:
                            pe.wait_ge(ks_in, 16 * K_LOADS)
                        if h == 0:
                            pe.wait_ge(qs_in[t % 2], 48 * (t // 2 + 1))
                        for i in range(2):
                            ins = pe.matmul(plan.room(("s", s))[:, i * 512:(i + 1) * 512], qstack[:, t % 2, h, :],
                                            kstack[:, h, i * 512:(i + 1) * 512], start=True, stop=True)
                        ins.then_inc(plan.full_sem(("s", s)), 1)

                    def turn_probs(s, i):
                        plan.free_of(pe, ("s", s))
                        for i in (i,):
                            plan.unit_clear(pe, ("t", s, i))
                            for k in range(4):
                                ins = pe.transpose(plan.room(("t", s, i))[:, k * P:(k + 1) * P],
                                                   prob[:, s % 2, (4 * i + k) * P:(4 * i + k + 1) * P], ident[:, :])
                            ins.then_inc(plan.full_sem(("t", s, i)), 1)

                    def attend(u, quarter):
                        g = u % 2
                        if quarter == 0:
                            plan.unit_clear(pe, ("pv", u))
                            plan.free_of(pe, ("t", 4 * u + 3, 0))
                            plan.free_of(pe, ("t", 4 * u + 3, 1))
                        for k in range(quarter * TT // 4, (quarter + 1) * TT // 4):
                            for h in range(4):
                                ins = pe.matmul(plan.room(("pv", u))[h * HD:(h + 1) * HD, 0:P],
                                                vtok[:, k, (4 * g + h) * HD:(4 * g + h + 1) * HD],
                                                pt[:, u % 2, h, k, :], start=(k == 0), stop=(k == TT - 1))
                        if quarter == 3:
                            ins.then_inc(plan.full_sem(("pv", u)), 1)

                    def turn_out(u):
                        plan.unit_clear(pe, ("otok", u))
                        plan.free_of(pe, ("pv", u))
                        pe.transpose(plan.room(("otok", u))[:, 0:P], ots[:, u % 2, :], ident[:, :]).then_inc(plan.full_sem(("otok", u)), 1)

                    def turn_back(u):
                        plan.free_of(pe, ("otok", u))
                        pe.transpose(plan.room(("ot", u))[:, 0:P], otok[:, u % 2, :, :].rearrange("p h d -> p (h d)"),
                                     ident[:, :]).then_inc(plan.full_sem(("ot", u)), 1)

                    def project(t):
                        key = ("wo", t)
                        plan.unit_clear(pe, key)
                        plan.free_of(pe, ("ot", 2 * t + 1))
                        pe.matmul(plan.room(key)[:, 0:D], ones[32:34, :], row_o, start=True, stop=False)
                        for k in range(KD):
                            ins = mm3(pe, plan.room(key)[:, 0:D], parts(act_t, k, slice(t * P, (t + 1) * P)), parts(w_at["o"], k), False,
                                      k == KD - 1)
                        ins.then_inc(plan.full_sem(key), 1)

                    def turn2(blk):
                        turn_rows(pe, plan, "z2", lambda i: z[:, i, :], blk, lambda i: pe.wait_ge(z2_ready, 4 * blk + i + 1))

                    def expand(c, m):
                        key = ("w1", c, m)
                        plan.unit_clear(pe, key)
                        for k in range(KD):
                            pe.wait_ge(split_done, plan.splits["z2", c // 2, k] + 1)
                            ins = mm3(pe, plan.room(key)[:, 0:256], parts(w_at["1"], k, slice(m * P, (m + 1) * P)),
                                      parts(n2_t, k, slice(c * 256, (c + 1) * 256)), k == 0, k == KD - 1)
                        ins.then_inc(plan.full_sem(key), 1)

                    def contract(t):
                        key = ("w2", t)
                        plan.unit_clear(pe, key)
                        pe.matmul(plan.room(key)[:, 0:D], ones[32:34, :], row_2, start=True, stop=False)
                        for m in range(FM):
                            pe.wait_ge(split_done, plan.splits["w1", t // 2, m] + 1)
                            ins = mm3(pe, plan.room(key)[:, 0:D], parts(wide, m, slice((t % 2) * P, (t % 2 + 1) * P)),
                                      parts(w_at["2"], m), False, m == FM - 1)
                        ins.then_inc(plan.full_sem(key), 1)

                    scores(0)
                    scores(1)
                    for s in range(SLOTS + 8):
                        if s + 2 < SLOTS:
                            scores(s + 2)
                        if 4 <= s < SLOTS + 4:
                            attend(s // 4 - 1, s % 4)
                        if s < SLOTS:
                            turn_probs(s, 0)
                            turn_probs(s, 1)
                        if s == SLOTS:
                            turn2(0)
                        for m in EARLY.get(s, ()):
                            expand(0, m)
                        if s % 4 == 0 and s >= 8:
                            turn_out((s - 8) // 4)
                        if s % 4 == 1 and s >= 9:
                            turn_back((s - 9) // 4)
                        if s % 8 == 7 and s >= 15:
                            project((s - 15) // 8)
                    for c in range(TT // 2):
                        if c >= 1:
                            for m in range(FM):
                                expand(c, m)
                        for t in (2 * c, 2 * c + 1):
                            contract(t)
                        if c == 0:
                            turn2(1)
                        if c == 1:
                            plan.unit_clear(pe, ("peak",))
                            pe.wait_ge(many_known, 1)
                            pe.transpose(plan.room(("peak",))[0:1, 0:P], peak[:, :], ident[:, :]).then_inc(plan.full_sem(("peak",)), 1)
                        if c == 2:
                            pe_hid(pe, plan, 0)

            nc.sync.sem_clear(span(carried_sems))
            has_many = nc.values_load(many[0:1, 0:1], min_val=0, max_val=1)
            with nc.If(has_many > 0):
                second_layer(every_label, LABELS, b_next, adjt_b, out_b, pool_steps, dve_steps)
            with nc.Else():
                second_layer(one_label, 1, b_next, adjt_b, out_b, pool_steps, dve_steps)

        with nc.Block() as block:
            @block.sync
            def _(sp):
                sp.wait_ge(y_out, 16 * TT)
                sp.wait_ge(ks_in, 16 * K_LOADS)
                sp.wait_ge(qs_in[0], 48)


def kernel(x, adj, L0_gnn_ln1_g, L0_gnn_ln1_b, L0_gnn_ln2_g, L0_gnn_ln2_b, L0_gnn_wq, L0_gnn_bq, L0_gnn_wk, L0_gnn_bk,
           L0_gnn_wv, L0_gnn_bv, L0_gnn_wo, L0_gnn_bo, L0_gnn_w1, L0_gnn_b1, L0_gnn_w2, L0_gnn_b2, L1_gnn_Wd, L1_gnn_bd,
           L1_gnn_Wri, L1_gnn_bri, L1_gnn_Wrh, L1_gnn_brh, L1_gnn_Wzi, L1_gnn_bzi, L1_gnn_Wzh, L1_gnn_bzh, L1_gnn_Wni,
           L1_gnn_bni, L1_gnn_Wnh, L1_gnn_bnh, L1_gnn_gamma, L1_gnn_beta):
    import concourse.bacc as bacc
    from concourse.bass_utils import run_bass_kernel_spmd

    turned = lambda w: np.ascontiguousarray(np.asarray(w).T)
    given = {
        "x": x, "adj": adj, "adj_t": np.ascontiguousarray(np.asarray(adj).transpose(0, 2, 1)),
        "ln1_g": L0_gnn_ln1_g, "ln1_b": L0_gnn_ln1_b, "ln2_g": L0_gnn_ln2_g, "ln2_b": L0_gnn_ln2_b,
        "wq": L0_gnn_wq, "bq": L0_gnn_bq, "wk": L0_gnn_wk, "bk": L0_gnn_bk, "wv": L0_gnn_wv, "bv": L0_gnn_bv,
        "wo": L0_gnn_wo, "bo": L0_gnn_bo, "w1": L0_gnn_w1, "b1": L0_gnn_b1, "w2": L0_gnn_w2, "b2": L0_gnn_b2,
        "wd_t": turned(L1_gnn_Wd), "bd": L1_gnn_bd,
        "wri_t": turned(L1_gnn_Wri), "bri": L1_gnn_bri, "wrh_t": turned(L1_gnn_Wrh), "brh": L1_gnn_brh,
        "wzi_t": turned(L1_gnn_Wzi), "bzi": L1_gnn_bzi, "wzh_t": turned(L1_gnn_Wzh), "bzh": L1_gnn_bzh,
        "wni_t": turned(L1_gnn_Wni), "bni": L1_gnn_bni, "wnh_t": turned(L1_gnn_Wnh), "bnh": L1_gnn_bnh,
        "gamma": L1_gnn_gamma, "beta": L1_gnn_beta,
    }
    nc = bacc.Bacc("TRN2", target_bir_lowering=False, num_devices=1)
    arrays, args = {}, []
    for name, a in given.items():
        a = np.ascontiguousarray(np.asarray(a))
        arrays[f"in_{name}"] = a
        args.append(nc.dram_tensor(f"in_{name}", a.shape, mybir.dt.from_np(a.dtype), kind="ExternalInput").ap())
    out = nc.dram_tensor("out_y", x.shape, F32, kind="ExternalOutput").ap()
    gated_graph_layers(nc, *args, out)
    r = run_bass_kernel_spmd(nc, [arrays], core_ids=[0])
    return r.results[0]["out_y"]
```
